# Optimizing a Trainium2 kernel written in Bass

```python
import numpy as np
import jax
import jax.numpy as jnp

def _softmax(x, axis=-1):
    return jax.nn.softmax(x, axis=axis)

def _gelu(x):
    return jax.nn.gelu(x, approximate=True)

def _silu(x):
    return jax.nn.silu(x)

def _sigmoid(x):
    return jax.nn.sigmoid(x)

def _layernorm(x, axis=-1, eps=1e-05):
    m = jnp.mean(x, axis=axis, keepdims=True)
    v = jnp.var(x, axis=axis, keepdims=True)
    return (x - m) / jnp.sqrt(v + eps)

def _scatter_add(tgt, idx, src, axis=0):
    return tgt.at[idx].add(src)

def _segment_sum(src, seg, n):
    return jax.ops.segment_sum(src, seg, n)
kernel_name = 'mk_conv_preact_d2_conv_nhwc512_r4_dd1042'

def setup_inputs(seed: int=0):
    np.random.seed(seed)
    _w = jnp.asarray

    def _rec_inputs():
        import jax
        import jax.numpy as jnp
        _gk = jax.random.key(seed)
        x = -0.0002091 + 1 * jax.random.normal(jax.random.fold_in(_gk, 1), (16, 28, 28, 128), jnp.float32)
        return x
    x = _rec_inputs()

    def _L0_conv_setup():
        import jax, jax.numpy as jnp
        import numpy as np
        from jax import lax
        NUM_GROUPS = 32
        key = jax.random.key(seed)
        kx, kw = jax.random.split(key)
        B, H, Wd, Cin = (16, 28, 28, 128)
        filters = 128
        x = jax.random.normal(kx, (B, H, Wd, Cin), dtype=jnp.float32)
        W = jax.random.normal(kw, (3, 3, Cin // NUM_GROUPS, filters), dtype=jnp.float32) * 0.05
        return {'x': x, 'W': W}
    _L0_conv_all = _L0_conv_setup()
    _L0_conv_in = {k: v for k, v in _L0_conv_all.items() if k in ('W',)}
    del _L0_conv_all

    def _L1_conv_setup():
        import jax, jax.numpy as jnp
        import numpy as np
        DIM = 128
        HEADS = 16
        HEAD_DIM = DIM // HEADS
        K = 7
        R = (K - 1) // 2
        SCALE = HEAD_DIM ** (-0.5)
        key = jax.random.key(seed)
        k0, k1, k2, k3 = jax.random.split(key, 4)
        x = jax.random.normal(k0, (8, 56, 56, DIM), jnp.float32)
        w_qkv = jax.random.normal(k1, (DIM, 3 * DIM), jnp.float32) * 0.02
        b_qkv = jnp.zeros((3 * DIM,), jnp.float32)
        rpb = jax.random.normal(k2, (HEADS, 2 * K - 1, 2 * K - 1), jnp.float32) * 0.02
        w_proj = jax.random.normal(k3, (DIM, DIM), jnp.float32) * 0.02
        b_proj = jnp.zeros((DIM,), jnp.float32)
        return {'x': x, 'w_qkv': w_qkv, 'b_qkv': b_qkv, 'rpb': rpb, 'w_proj': w_proj, 'b_proj': b_proj}
    _L1_conv_all = _L1_conv_setup()
    _L1_conv_in = {k: v for k, v in _L1_conv_all.items() if k in ('w_qkv', 'b_qkv', 'rpb', 'w_proj', 'b_proj')}
    del _L1_conv_all
    return {'x': x, 'L0_conv_W': _L0_conv_in['W'], 'L1_conv_w_qkv': _L1_conv_in['w_qkv'], 'L1_conv_b_qkv': _L1_conv_in['b_qkv'], 'L1_conv_rpb': _L1_conv_in['rpb'], 'L1_conv_w_proj': _L1_conv_in['w_proj'], 'L1_conv_b_proj': _L1_conv_in['b_proj']}

def reference(x, L0_conv_W, L1_conv_w_qkv, L1_conv_b_qkv, L1_conv_rpb, L1_conv_w_proj, L1_conv_b_proj):
    import jax
    import jax.numpy as jnp

    def _L0_conv_ref(x, W):
        import jax, jax.numpy as jnp
        import numpy as np
        from jax import lax
        NUM_GROUPS = 32
        return lax.conv_general_dilated(x, W, window_strides=(1, 1), padding='SAME', dimension_numbers=('NHWC', 'HWIO', 'NHWC'), feature_group_count=NUM_GROUPS)

    def _L1_conv_ref(x, w_qkv, b_qkv, rpb, w_proj, b_proj):
        import jax, jax.numpy as jnp
        import numpy as np
        DIM = 128
        HEADS = 16
        HEAD_DIM = DIM // HEADS
        K = 7
        R = (K - 1) // 2
        SCALE = HEAD_DIM ** (-0.5)
        B, H, W, C = x.shape
        qkv = (x @ w_qkv + b_qkv).reshape(B, H, W, 3, HEADS, HEAD_DIM)
        qkv = jnp.transpose(qkv, (3, 0, 4, 1, 2, 5))
        q, k, v = (qkv[0] * SCALE, qkv[1], qkv[2])
        start_h = jnp.clip(jnp.arange(H) - R, 0, H - K)
        start_w = jnp.clip(jnp.arange(W) - R, 0, W - K)
        qi_h = jnp.arange(H)
        qi_w = jnp.arange(W)
        logits = []
        for a in range(K):
            ih = start_h + a
            bh = ih + (K - 1) - qi_h
            for b in range(K):
                iw = start_w + b
                bw = iw + (K - 1) - qi_w
                ks = k[:, :, ih][:, :, :, iw]
                bias = rpb[:, bh][:, :, bw]
                logits.append(jnp.einsum('bnhwd,bnhwd->bnhw', q, ks) + bias[None])
        logits = jnp.stack(logits, axis=-1)
        attn = jax.nn.softmax(logits, axis=-1)
        out = jnp.zeros_like(q)
        i = 0
        for a in range(K):
            ih = start_h + a
            for b in range(K):
                iw = start_w + b
                vs = v[:, :, ih][:, :, :, iw]
                out = out + attn[..., i, None] * vs
                i += 1
        out = jnp.transpose(out, (0, 2, 3, 1, 4)).reshape(B, H, W, C)
        return out @ w_proj + b_proj

    def _gn(v, G=32, eps=1e-05):
        B_, H_, W_, C_ = v.shape
        g = v.reshape(B_, H_, W_, G, C_ // G)
        m = jnp.mean(g, axis=(1, 2, 4), keepdims=True)
        s = jnp.var(g, axis=(1, 2, 4), keepdims=True)
        return ((g - m) / jnp.sqrt(s + eps)).reshape(v.shape)

    def _ln_c(v, eps=1e-06):
        m = jnp.mean(v, axis=-1, keepdims=True)
        s = jnp.var(v, axis=-1, keepdims=True)
        return (v - m) / jnp.sqrt(s + eps)

    def _ln_t(v, eps=1e-05):
        m = jnp.mean(v, axis=-1, keepdims=True)
        s = jnp.var(v, axis=-1, keepdims=True)
        return (v - m) / jnp.sqrt(s + eps)

    def _to_tokens(v):
        B_, H_, W_, C_ = v.shape
        return v.reshape(B_, H_ * W_, C_)

    def _from_tokens(t, like):
        return t.reshape(like.shape)
    x = x + _L0_conv_ref(_gn(x), L0_conv_W)
    x = x + _L1_conv_ref(_gn(x), L1_conv_w_qkv, L1_conv_b_qkv, L1_conv_rpb, L1_conv_w_proj, L1_conv_b_proj)
    return x

_drawn_inputs = setup_inputs


def setup_inputs(seed=0):
    import zlib

    import numpy as np

    out = dict(_drawn_inputs(seed))
    spreads = {'L1_conv_b_qkv': (0.0, 0.416), 'L1_conv_b_proj': (0.0, 0.1)}
    factors = {'L1_conv_w_qkv': 8.0, 'L1_conv_rpb': 8.0, 'L1_conv_w_proj': 2.697}
    for name, (base, spread) in spreads.items():
        noise = np.random.default_rng([zlib.crc32(name.encode()), seed]).standard_normal(out[name].shape)
        drawn = base * np.exp(spread * noise) if base else spread * noise
        out[name] = jnp.asarray(drawn.astype(out[name].dtype))
    for name, factor in factors.items():
        out[name] = (out[name] * factor).astype(out[name].dtype)
    return out
```

```python
from contextlib import ExitStack

import concourse.bass as bass
from concourse import mybir

IMAGES, SIDE, CH = 16, 28, 128
POS = SIDE * SIDE
HEADS, HEAD_DIM = 16, 8
WIN, REACH = 7, 3
TABLE = 2 * WIN - 1
HALF = POS // 2
HALF_ROWS = SIDE // 2
NORM_GROUP = 4
PAD = SIDE + 2
PIECES, PIECE = 7, POS // 7

PATCH = 8
ROWS_OF_PATCHES = SIDE // 2
OUTER_PATCHES = 3 * ROWS_OF_PATCHES
MIDDLE_PATCHES = ROWS_OF_PATCHES // 2
PATCHES = OUTER_PATCHES + MIDDLE_PATCHES
CHUNK_Q = PATCH * PATCHES
TILES = 16

OUTER_W, MIDDLE_W, MIDDLE_COL = 16, 10, 9
OUTER_COL = (0, SIDE - OUTER_W)
STRIP = PAD * OUTER_W
MIDDLE_AT = 2 * STRIP
KEYS = MIDDLE_AT + 320
WINDOWS = 14

OUTER_KINDS = (0, 1, 2, 12, 13)
NEG = -1.0e30

CHUNK_BANKS = 9
PATCH_KEYS = 80
BIAS_PATCHES = 25


def outer_window(rt):
    return min(max(rt - 1, 0), 11)


def tile_of(a, n):
    if n < ROWS_OF_PATCHES:
        u = outer_window(n)
        return 3 * n, 3, a * STRIP + 2 * u * OUTER_W, u
    first, count, row = middle_tile(a, n)
    return first, count, MIDDLE_AT + (row + 1) * MIDDLE_W, n - 2


def middle_tile(a, n):
    return {(0, 14): (42, 4, 0), (0, 15): (46, 3, 5), (1, 14): (42, 3, 11), (1, 15): (45, 4, 17)}[a, n]


def bias_kinds(a):
    out, at = [], a * BIAS_COLS // 2
    for n in (*OUTER_KINDS, 14, 15):
        count = tile_of(a, n)[1]
        out.append((n, at, count))
        at += HEADS * PATCH * count
    return out


BIAS_COLS = 2 * HEADS * PATCH * (3 * len(OUTER_KINDS) + MIDDLE_PATCHES)


def bias_at(a, n):
    kind = n if n in (0, 1, 12, 13, 14, 15) else 2
    return next(at for m, at, _ in bias_kinds(a) if m == kind)


def kind_of_row(rt):
    return OUTER_KINDS.index(rt if rt in OUTER_KINDS else 2)


def patch_bank(a, b):
    if b < 7:
        return 6 * b, 6, (0 if b == 0 else 12 if b == 6 else 6)
    n = 14 + b - 7
    first, count, _ = middle_tile(a, n)
    return first, count, 18 + first - OUTER_PATCHES


def patch_keys(a, t):
    if t >= OUTER_PATCHES:
        rt = MIDDLE_PATCHES * a + t - OUTER_PATCHES
        return MIDDLE_AT + 2 * outer_window(rt) * MIDDLE_W, MIDDLE_W
    rt, j = divmod(t, 3)
    return a * STRIP + 2 * outer_window(rt) * OUTER_W + PATCH_COL[a][j], OUTER_W


PATCH_COL = ((0, 1, 5), (1, 5, 6))

LEFT, WHOLE, RIGHT = (0, 0, 0), (0, 1, 1), (1, 2, 6)
PATCH_SOURCES = [(r, source) for r in range(len(OUTER_KINDS)) for source in (LEFT, WHOLE, RIGHT)]


def patch_source(a, i):
    if i >= 18:
        return kind_of_row(MIDDLE_PATCHES * a + i - 18), WHOLE
    r, j = divmod(i, 3)
    return (0, 1, 2, 2, 3, 4)[r], {(0, 0): LEFT, (1, 2): RIGHT}.get((a, j), WHOLE)

SEL_OUTER = TABLE * OUTER_W
SEL_MIDDLE_FIRST = -4
SEL_MIDDLE = 24 * MIDDLE_W
SEL_COLS = 24 * SEL_OUTER + 4 * SEL_MIDDLE
TABLE_SPLIT = 7
TABLE_PARTS = (TABLE_SPLIT * TABLE, (TABLE - TABLE_SPLIT) * TABLE)


def query_of(a, n, q, j):
    r, c = divmod(q, 4)
    if n < ROWS_OF_PATCHES:
        return 2 * n + r, 16 * a + 4 * j + c
    first = middle_tile(a, n)[0] - OUTER_PATCHES
    return 2 * (MIDDLE_PATCHES * a + first + j) + r, 12 + c


def selection_at(a, n, q, j):
    row, col = query_of(a, n, q, j)
    if n < ROWS_OF_PATCHES:
        first = 2 * outer_window(n) - 1
        return (12 * a + col - 16 * a) * SEL_OUTER + (first - row + WIN - 1) * OUTER_W
    first = middle_tile(a, n)[2]
    return 24 * SEL_OUTER + (col - 12) * SEL_MIDDLE + (first - row + WIN - 1 - SEL_MIDDLE_FIRST) * MIDDLE_W


C_ID, C_GROUP, C_HEAD, C_OUT, CONSTS = 0, 128, 256, 272, 276


BF16_ONE = 0x3F80


def constants():
    import numpy as np

    c = np.zeros((128, CONSTS), np.float32)
    window = np.zeros((128, BIAS_COLS // HEADS), np.float32)
    p = np.arange(128)
    c[:, C_ID:C_ID + 128] = np.eye(128)
    c[:, C_GROUP:C_GROUP + 128] = p[:, None] // NORM_GROUP == p[None] // NORM_GROUP
    c[:, C_HEAD:C_HEAD + HEADS] = p[:, None] // HEAD_DIM == np.arange(HEADS)[None]
    c[:, C_OUT:C_OUT + 4] = p[:, None] % 32 // HEAD_DIM == np.arange(4)[None]
    for a in range(2):
        for n, at, count in bias_kinds(a):
            if n < ROWS_OF_PATCHES:
                krow, kcol = 2 * outer_window(n) - 1 + p // OUTER_W, OUTER_COL[a] + p % OUTER_W
            else:
                krow, kcol = middle_tile(a, n)[2] + p // MIDDLE_W, MIDDLE_COL + p % MIDDLE_W
            for q in range(PATCH):
                for j in range(count):
                    row, col = query_of(a, n, q, j)
                    r0, c0 = (min(max(z - REACH, 0), SIDE - WIN) for z in (row, col))
                    seen = (krow >= r0) & (krow < r0 + WIN) & (kcol >= c0) & (kcol < c0 + WIN)
                    window[:, at // HEADS + q * count + j] = np.where(seen, 0.0, NEG)
    sel = np.zeros((2, 128, SEL_COLS), np.float32)
    for dh in range(TABLE):
        for dw in range(TABLE):
            part, entry = (0, dh * TABLE + dw) if dh < TABLE_SPLIT else (1, (dh - TABLE_SPLIT) * TABLE + dw)
            for a in range(2):
                for c12 in range(12):
                    k = dw - (WIN - 1) + 16 * a + c12 - OUTER_COL[a]
                    if 0 <= k < OUTER_W:
                        sel[part, entry, (12 * a + c12) * SEL_OUTER + dh * OUTER_W + k] = 1
            for c4 in range(4):
                k = dw - (WIN - 1) + 12 + c4 - MIDDLE_COL
                if 0 <= k < MIDDLE_W:
                    sel[part, entry, 24 * SEL_OUTER + c4 * SEL_MIDDLE + (dh - SEL_MIDDLE_FIRST) * MIDDLE_W + k] = 1
    return c, window, (sel * BF16_ONE).astype(np.uint16)


def build(nc, x, conv_w, w_qkv, b_qkv, rpb, w_proj, b_proj, const, window, select, out):
    F32, BF16 = mybir.dt.float32, mybir.dt.bfloat16
    ALU, ACT, AX = mybir.AluOpType, mybir.ActivationFunctionType, mybir.AxisListType
    SCALE = float(HEAD_DIM) ** -0.5

    ctx = ExitStack()
    with ctx:
        def sb(name, shape, dt=F32):
            return ctx.enter_context(nc.sbuf_tensor(name, shape, dt))

        cst = sb("cst", [128, CONSTS])
        identb = sb("identb", [128, 128], BF16)
        wqkv = sb("wqkv", [128, 3 * CH])
        bqkv = sb("bqkv", [128, 3])
        wproj = sb("wproj", [128, 2, CH])
        bproj = sb("bproj", [128, 1])
        minus = sb("minus", [33, 128], BF16)
        X = sb("X", [128, IMAGES, POS])
        mv = sb("mv", [128, IMAGES, 2])
        small = sb("small", [128, 7, IMAGES])
        bias = sb("bias", [128, BIAS_COLS])
        biasp = sb("biasp", [128, 2, BIAS_PATCHES, PATCH_KEYS], BF16)

        K = [sb(f"K{i}", [128, KEYS]) for i in range(2)]
        V = [sb(f"V{i}", [128, KEYS]) for i in range(2)]
        qs = sb("qs", [128, 2, PATCH, PATCHES])
        mcol = sb("mcol", [128, PATCHES], BF16)
        mrow = sb("mrow", [33, HEADS * PATCH * PATCHES], BF16)
        S = sb("S", [128, 4, 512])
        VT = sb("VT", [128, 4, 4, 64])
        masked = sb("masked", [128, 2, 256])
        halves = sb("halves", [128, 2, 128])
        sel = sb("sel", [128, 2, 2, PATCH, PATCHES])
        den = sb("den", [128, 2 * CHUNK_Q])
        normed = sb("normed", [128, 2 * CHUNK_Q])
        xn = sb("xn", [128, POS])
        yo = sb("yo", [128, POS])
        ot = sb("ot", [PIECE, PIECES, CH])
        Qbd = [sb(f"Qbd{i}", [128, HEADS, PATCH, PATCHES]) for i in range(2)]
        space = [Qbd[i][:, :, :, :].rearrange("p h q t -> p (h q t)") for i in range(2)]
        wconv = space[0][:, 0:9 * CH].rearrange("p (t c) -> p t c", t=9)
        padded = [space[0][:, 1152 + i * 900:2052 + i * 900] for i in range(2)]
        xin = [space[0][0:PIECE, 2952 + i * 896:3848 + i * 896].rearrange("p (k c) -> p k c", k=PIECES) for i in range(2)]
        chosen = [space[1][:, i * SEL_COLS // 2:(i + 1) * SEL_COLS // 2].bitcast(BF16) for i in range(2)]
        seen = space[0][:, 4744:4744 + BIAS_COLS // HEADS]
        stats = yo[:, 0:12 * IMAGES].rearrange("p (i k) -> p i k", k=12)
        table = [sel[0:TABLE_PARTS[i], 0, i, 0, 0:HEADS] for i in range(2)]
        tparts = [masked[0:TABLE_PARTS[i], i, 0:24].bitcast(BF16) for i in range(2)]
        trest = [halves[0:TABLE_PARTS[i], i, 0:HEADS] for i in range(2)]
        biasb = [S[:, 0, 64 * i:64 * i + 64].bitcast(BF16) for i in range(8)]

        KINDS = [(a, n, at, count) for a in range(2) for n, at, count in bias_kinds(a)]

        def turned_bias(k):
            return PS[:, k % 8, 0:64].bitcast(BF16)

        PS = ctx.enter_context(nc.psum_tensor("PS", [128, 8, 512], F32))
        SCORE, SUM, VALUE, PEAK, MISC = 0, 2, 4, 6, 7

        CREDIT = {"xin_kept": 2, "conv_added": 4, "weighted": 4, "selected": 2, "half": 2,
                  "value_out": 1, "summed": 1, "normed": 1, "out_done": 1, "qbd": 1}
        EACH = {"misc_in": 20, "misc_out": 20, "mrow": 64, "scores": 64, "biased": 64, "probs": 64,
                "weighted": 64, "selected": 64, "half": 64, "summed": 64, "qbd": 4, "peak_in": 4 * CHUNK_BANKS,
                "peak_out": 4 * CHUNK_BANKS, "value_in": 4 * WINDOWS, "value_out": 4 * WINDOWS,
                "den_in": 128, "recip": 4, "normed": 4, "residual": 2, "out_done": 32, "xn_ready": 2}
        s = {name: ctx.enter_context(nc.semaphore("s_" + name)) for name in (
            *EACH, "init", "cleared", "pool_loaded", "const_in", "loaded", "xin_in0", "xin_in1", "xin_turned", "xin_kept", "table_in", "table_split",
            "table_picked", "table_kept", "rounded", "turned", "placed", "dve_chain", "mean_in", "mean_sum", "var_in",
            "var_sum", "sqrt_in", "sqrt_out", "padded_ready", "conv", "conv_added", "first_stats")}

        def wait(eng, name, k, j=None, each=None):
            k += CREDIT.get(name, 0)
            assert k >= 0 if j is None else k > 0, (name, k)
            eng.wait_ge(s[name], k if j is None else j * (each or EACH[name]) + k)

        ident, group = cst[:, C_ID:C_ID + 128], cst[:, C_GROUP:C_GROUP + 128]
        MEAN, RSTD = 0, 1
        INITS = 17
        SMALL_LOADS, POOL_LOADS = 16 * 3, 16 * (4 + 32 + 2 + 1)
        MISC_IMAGE, MISC_FIRST = 10, 6
        block = ctx.enter_context(nc.Block())

        MISC_PROJECT, MISC_QKV, MISC_TURN = 6, 7, 13
        SPREAD = {0: range(0, 6), 1: range(6, 11), 2: range(11, 16)}
        FIRST_BANK, NORMALIZE, NEXT_IMAGE = 3, 5, 4

        def misc_project(c):
            return MISC_FIRST + MISC_IMAGE * (c // 2) + (0 if c % 2 == 0 else 9)

        def misc_qkv(i, which, half):
            return (MISC_IMAGE * (i - 1) + MISC_FIRST + 1 if i else 0) + 2 * which + half

        def misc_turn(i, part):
            return MISC_FIRST + MISC_IMAGE * i + (7 if i < IMAGES else 1) + part

        def new_window(n):
            w = tile_of(0, n)[3]
            return w if n == 0 or tile_of(0, n - 1)[3] != w else None

        def window_for_next(c, n):
            c, n = (c, n + 1) if n + 1 < TILES else (c + 1, 0)
            w = new_window(n)
            return None if w is None else (c, n, WINDOWS * c + w)

        def tiles_until(w):
            c, k = divmod(w, WINDOWS)
            return TILES * c + max(n for n in range(TILES) if tile_of(0, n)[3] == k) + 1

        @block.sync
        def _(sp):
            for b in range(2):
                sp.dma_start(xin[b], x[b].rearrange("(k p) c -> p k c", p=PIECE)).then_inc(s[f"xin_in{b}"], 16)
            sp.dma_start(cst[:, :], const).then_inc(s["const_in"], 16)
            sp.dma_start(wqkv[:, :], w_qkv).then_inc(s["loaded"], 16)
            sp.dma_start(bqkv[:, :], b_qkv.rearrange("(k p) -> p k", p=128),
                         allow_slow_non_contiguous=True).then_inc(s["loaded"], 16)
            sp.dma_start(bproj[:, :], b_proj.rearrange("(p o) -> p o", o=1)).then_inc(s["loaded"], 16)
            with nc.sync.Fori(0, IMAGES // 2 - 1) as j:
                for b in range(2):
                    wait(sp, "xin_turned", b + 1, j, 2)
                    sp.dma_start(xin[b], x[2 * j + 2 + b].rearrange("(k p) c -> p k c", p=PIECE)).then_inc(s[f"xin_in{b}"], 16)

            def move_maxima(j, c):
                wait(sp, "peak_out", (c + 1) * CHUNK_BANKS, j)
                row = 32 * (c % 2)
                sp.dma_start(mrow[row:row + 1, :].rearrange("o (p t) -> o p t", p=128), mcol[:, :]).then_inc(s["mrow"], 16)

            def move_denominators(j, c):
                wait(sp, "summed", TILES * c, j)
                for g in range(2):
                    sp.dma_start(den[64 * g:64 * g + 32, :],
                                 sel[64 * g + 32:64 * g + 64, (c + 1) % 2, :, :, :].rearrange("p g q t -> p (g q t)")
                                 ).then_inc(s["den_in"], 16)

            def store(j, i, img):
                wait(sp, "misc_out", misc_turn(i, 1) + 1, j)
                sp.dma_start(out[img].rearrange("(k p) c -> p k c", p=PIECE), ot[:, :, :]).then_inc(s["out_done"], 16)

            sp.wait_ge(s["init"], INITS)
            move_maxima(None, 0)
            with nc.sync.Fori(0, IMAGES // 2) as j:
                for c in range(4):
                    move_denominators(j, c)
                    move_maxima(j, c + 1)
                    if c % 2 == 0:
                        store(j, c // 2, (2 * j + c // 2 + IMAGES - 1) % IMAGES)
            move_denominators(None, 2 * IMAGES)
            store(None, IMAGES, IMAGES - 1)
            wait(sp, "out_done", 16 * (IMAGES + 1))

        @block.gpsimd
        def _(pool):
            nc.gpsimd.memset(wproj[:, :, :], 0.0).then_inc(s["cleared"], 1)
            for ap, value in ((minus[:, :], -1.0), (padded[0], 0.0), (padded[1], 0.0),
                              (den[:, :], 1.0), (K[0][:, :], 0.0), (K[1][:, :], 0.0), (V[0][:, :], 0.0), (V[1][:, :], 0.0)):
                nc.gpsimd.memset(ap, value).then_inc(s["init"], 1)
            pool.wait_ge(s["cleared"], 1)
            for g in range(4):
                pool.dma_start(wproj[64 * (g % 2):64 * (g % 2) + 32, g // 2, :], w_proj[32 * g:32 * g + 32, :]
                               ).then_inc(s["pool_loaded"], 16)
            for g in range(CH // NORM_GROUP):
                pool.dma_start(wconv[4 * g:4 * g + 4, :, :], conv_w.rearrange("a b j o -> j (a b) o")
                               ).then_inc(s["pool_loaded"], 16)
            for i in range(2):
                pool.dma_start(chosen[i], select[i].bitcast(BF16)).then_inc(s["pool_loaded"], 16)
            pool.dma_start(seen, window).then_inc(s["pool_loaded"], 16)
            for i in range(2):
                first = TABLE_SPLIT * i
                rows = rpb[:, first:first + TABLE_PARTS[i] // TABLE, :]
                pool.dma_start(table[i], rows.rearrange("h a b -> (a b) h"), allow_slow_non_contiguous=True).then_inc(s["table_in"], 16)
            pool.wait_ge(s["table_kept"], 14)
            nc.gpsimd.memset(sel[:, :, :, :, :], 1.0).then_inc(s["init"], 1)
            nc.gpsimd.memset(yo[:, :], 0.0).then_inc(s["init"], 1)
            pool.wait_ge(s["init"], INITS)

            def add_heads(j, c, n):
                t0, count, _, _ = tile_of(c % 2, n)
                T = TILES * c + n
                q = PATCH * count
                wait(pool, "selected", T + 1, j)
                if n == 0:
                    wait(pool, "normed", c, j)
                m = masked[:, n % 2, 0:8 * q].rearrange("p (g h q) -> p g h q", g=2, h=4)
                h = halves[:, n % 2, 0:4 * q].rearrange("p (g h q) -> p g h q", g=2, h=2)
                nc.gpsimd.tensor_tensor(h, m[:, :, 0:2, :], m[:, :, 2:4, :], ALU.add).then_inc(s["half"], 1)
                wait(pool, "half", T + 1, j)
                h = halves[:, n % 2, 0:4 * q].rearrange("p (g h a t) -> p g h a t", g=2, h=2, a=PATCH)
                nc.gpsimd.tensor_tensor(sel[:, c % 2, :, :, t0:t0 + count], h[:, :, 0], h[:, :, 1], ALU.add
                                        ).then_inc(s["summed"], 1)

            def add_residual(j, i, img):
                wait(pool, "misc_out", misc_project(2 * i) + 1, j)
                nc.gpsimd.tensor_tensor(yo[:, :], yo[:, :], X[:, img, :], ALU.add).then_inc(s["residual"], 1)

            with nc.gpsimd.Fori(0, IMAGES // 2) as j:
                for c in range(4):
                    for n in range(TILES):
                        add_heads(j, c, n)
                        if c % 2 == 0 and n == MISC_QKV + 1:
                            add_residual(j, c // 2, (2 * j + c // 2 + IMAGES - 1) % IMAGES)
            add_residual(None, IMAGES, IMAGES - 1)

        @block.scalar
        def _(act):
            with nc.scalar.Fori(0, IMAGES // 2) as j:
                for b in range(2):
                    wait(act, "xin_turned", b + 1, j, 2)
                    nc.scalar.activation(X[:, 2 * j + b, 0:448], PS[:, 2 * b, 0:448], ACT.Copy)
                    nc.scalar.activation(X[:, 2 * j + b, 448:784], PS[:, 2 * b + 1, 0:336], ACT.Copy
                                         ).then_inc(s["xin_kept"], 1)
            for k in range(2):
                act.wait_ge(s["sqrt_in"], k + 1)
                nc.scalar.activation(small[:, 4, :], small[:, 3, :], ACT.Sqrt).then_inc(s["sqrt_out"], 1)
            act.wait_ge(s["loaded"], SMALL_LOADS)
            nc.scalar.mul(bqkv[:, 0:1], bqkv[:, 0:1], SCALE).then_inc(s["init"], 1)

            def misc(j, k):
                wait(act, "misc_in", k + 1, j)
                return PS[:, MISC, 0:HALF]

            def keep(dst, src, func, **kw):
                for d, p in zip(dst, src):
                    last = nc.scalar.activation(d, p, func, **kw)
                last.then_inc(s["misc_out"], 1)

            def keep_qkv(j, i, which, half):
                p = misc(j, misc_qkv(i, which, half)).rearrange("p (r c) -> p r c", c=SIDE)
                if which == 0:
                    dst, src = [], []
                    pr = p.rearrange("p (t r) c -> p t r c", r=2)
                    for r in range(2):
                        for a in range(2):
                            o = qs[:, a, 4 * r:4 * r + 4, 21 * half:21 * half + 21]
                            dst.append(o.rearrange("p c (t j) -> p t j c", j=3))
                            src.append(pr[:, :, r, 16 * a:16 * a + 12].rearrange("p t (j c) -> p t j c", j=3))
                        dst.append(qs[:, half, 4 * r:4 * r + 4, OUTER_PATCHES:PATCHES].rearrange("p c t -> p t c"))
                        src.append(pr[:, :, r, 12:16])
                    if j is not None and half == 0:
                        wait(act, "qbd", 2 * i, j)
                    keep(dst, src, ACT.Identity, scale=SCALE, bias=bqkv[:, 0:1])
                    return
                buf = (K, V)[which - 1][i % 2]
                rows = slice(1 + HALF_ROWS * half, 1 + HALF_ROWS * (half + 1))
                strips = [(0, STRIP, OUTER_W, OUTER_COL[0]), (STRIP, STRIP, OUTER_W, OUTER_COL[1]),
                          (MIDDLE_AT, PAD * MIDDLE_W, MIDDLE_W, MIDDLE_COL)]
                dst = [buf[:, at:at + size].rearrange("p (r c) -> p r c", c=w)[:, rows, :] for at, size, w, _ in strips]
                src = [p[:, :, col:col + w] for _, _, w, col in strips]
                keep(dst, src, ACT.Identity, bias=bqkv[:, which:which + 1])

            def keep_value(j, w):
                wait(act, "value_in", w + 1, j)
                if j is not None:
                    wait(act, "weighted", tiles_until(w - 4), j)
                nc.scalar.activation(VT[:, w % 4, :, 0:32],
                                     PS[:, VALUE + w % 2, 0:128].rearrange("p (g c) -> p g c", g=4),
                                     ACT.Copy).then_inc(s["value_out"], 1)

            def exponentials(j, c, n):
                cols = HEADS * PATCH * tile_of(c % 2, n)[1]
                wait(act, "biased", TILES * c + n + 1, j)
                nc.scalar.activation(S[:, n % 4, 0:cols], S[:, n % 4, 0:cols], ACT.Exp).then_inc(s["probs"], 1)

            def keep_projection(j, c):
                a = (c + 1) % 2
                p = misc(j, misc_project(c)).rearrange("p (q t) -> p q t", q=PATCH)
                img = yo[:, :].rearrange("p (t r c) -> p t r c", r=2, c=SIDE)
                dst, src = [], []
                for r in range(2):
                    for half in range(2):
                        dst.append(img[:, 7 * half:7 * half + 7, r, 16 * a:16 * a + 12].rearrange("p t (j c) -> p t j c", j=3))
                        src.append(p[:, 4 * r:4 * r + 4, 21 * half:21 * half + 21].rearrange("p c (t j) -> p t j c", j=3))
                    dst.append(img[:, 7 * a:7 * a + 7, r, 12:16])
                    src.append(p[:, 4 * r:4 * r + 4, OUTER_PATCHES:PATCHES].rearrange("p c t -> p t c"))
                keep(dst, src, ACT.Identity, bias=bproj[:, 0:1])

            def keep_turned(j, i, part):
                misc(j, misc_turn(i, part))
                if part == 0:
                    wait(act, "out_done", 16 * i, j)
                count = 4 - part
                keep([ot[:, 4 * part:4 * part + count, :]],
                     [PS[0:PIECE, MISC, 0:CH * count].rearrange("p (k c) -> p k c", c=CH)], ACT.Copy)

            act.wait_ge(s["init"], INITS)
            for which in range(3):
                for half in range(2):
                    keep_qkv(None, 0, which, half)
            keep_value(None, 0)
            with nc.scalar.Fori(0, IMAGES // 2) as j:
                for c in range(4):
                    for n in range(TILES):
                        exponentials(j, c, n)
                        window = window_for_next(c, n)
                        if window:
                            keep_value(j, window[2])
                        if n == MISC_PROJECT:
                            keep_projection(j, c)
                        if c % 2 == 0 and MISC_QKV <= n < MISC_QKV + 6:
                            keep_qkv(j, c // 2 + 1, (n - MISC_QKV) // 2, (n - MISC_QKV) % 2)
                        if c % 2 == 0 and MISC_TURN <= n < MISC_TURN + 2:
                            keep_turned(j, c // 2, n - MISC_TURN)
            keep_projection(None, 2 * IMAGES)
            for part in range(2):
                keep_turned(None, IMAGES, part)

        @block.vector
        def _(dve):
            dve_steps = [0]

            def link(ins):
                dve_steps[0] += 1
                ins.then_inc(s["dve_chain"], 1)
                dve.wait_ge(s["dve_chain"], dve_steps[0])

            for w in range(4):
                nc.vector.memset(VT[:, w, :, :], 1.0).then_inc(s["init"], 1)
            for i, (name, credit) in enumerate(CREDIT.items()):
                nc.vector.memset(small[:, 6, i:i + 1], 0.0).then_inc(s[name], credit)
            dve.wait_ge(s["const_in"], 16)
            nc.vector.tensor_copy(identb[:, :], ident).then_inc(s["init"], 1)

            with nc.vector.Fori(0, IMAGES // 2) as j:
                for b in range(2):
                    wait(dve, "xin_kept", b + 1, j, 2)
                    for half in range(2):
                        nc.vector.bn_stats(stats[:, 2 * j + b, 6 * half:6 * half + 6],
                                           X[:, 2 * j + b, HALF * half:HALF * half + HALF]).then_inc(s["first_stats"], 1)

            def group_norm_terms(k, stats_done):
                dve.wait_ge(s["first_stats"], stats_done)
                for i in range(IMAGES):
                    last = nc.vector.bn_aggr(mv[:, i, :], stats[:, i, :].rearrange("p (h k) -> p h k", k=6))
                last.then_inc(s["mean_in"], 1)
                dve.wait_ge(s["mean_sum"], k + 1)
                link(nc.vector.tensor_scalar(small[:, MEAN, :], PS[:, PEAK, 0:IMAGES], 1.0 / NORM_GROUP, None, ALU.mult))
                dve.wait_ge(s["mean_in"], k + 1)
                link(nc.vector.tensor_tensor(small[:, 2, :], mv[:, :, 0], small[:, MEAN, :], ALU.subtract))
                link(nc.vector.tensor_tensor(small[:, 3, :], small[:, 2, :], small[:, 2, :], ALU.mult))
                nc.vector.tensor_tensor(small[:, 2, :], small[:, 3, :], mv[:, :, 1], ALU.add).then_inc(s["var_in"], 1)
                dve.wait_ge(s["var_sum"], k + 1)
                nc.vector.tensor_scalar(small[:, 3, :], PS[:, PEAK, 0:IMAGES], 1.0 / NORM_GROUP, 1e-5, ALU.mult, ALU.add
                                        ).then_inc(s["sqrt_in"], 1)
                dve.wait_ge(s["sqrt_in"], k + 1)
                dve.wait_ge(s["sqrt_out"], k + 1)
                link(nc.vector.reciprocal(small[:, 5, :], small[:, 4, :]))
                link(nc.vector.tensor_tensor(small[:, 6, :], small[:, 5, :], small[:, 5, :], ALU.mult))
                link(nc.vector.tensor_tensor(small[:, 6, :], small[:, 6, :], small[:, 3, :], ALU.mult))
                link(nc.vector.tensor_scalar(small[:, 6, :], small[:, 6, :], -0.5, 1.5, ALU.mult, ALU.add))
                link(nc.vector.tensor_tensor(small[:, RSTD, :], small[:, 5, :], small[:, 6, :], ALU.mult))

            def normalize(dst, img, done):
                nc.vector.tensor_scalar(dst, X[:, img, :].rearrange("p (r c) -> p r c", c=SIDE),
                                        small[:, MEAN, :].unsqueeze(2)[:, img, :], small[:, RSTD, :].unsqueeze(2)[:, img, :],
                                        ALU.subtract, ALU.mult).then_inc(s[done], 1)

            group_norm_terms(0, 2 * IMAGES)

            dve.wait_ge(s["init"], 13)
            inner = [padded[b].rearrange("p (r c) -> p r c", c=PAD)[:, 1:1 + SIDE, 1:1 + SIDE] for b in range(2)]
            dve.wait_ge(s["pool_loaded"], POOL_LOADS)
            link(nc.vector.tensor_tensor(wconv, wconv, group.unsqueeze(1).broadcast_to([128, 9, CH]), ALU.mult))
            normalize(inner[0], 0, "padded_ready")
            normalize(inner[1], 1, "padded_ready")
            with nc.vector.Fori(0, IMAGES // 2) as j:
                for b in range(2):
                    for half in range(2):
                        wait(dve, "conv", 2 * b + half + 1, j, 4)
                        xh = X[:, 2 * j + b, HALF * half:HALF * half + HALF]
                        nc.vector.tensor_tensor(xh, xh, PS[:, 2 * b + half, 0:HALF], ALU.add).then_inc(s["conv_added"], 1)
                    normalize(inner[b], (2 * j + b + 2) % IMAGES, "padded_ready")
                    for half in range(2):
                        wait(dve, "conv_added", 2 * b + half + 1, j, 4)
                        xh = X[:, 2 * j + b, HALF * half:HALF * half + HALF]
                        nc.vector.bn_stats(stats[:, 2 * j + b, 6 * half:6 * half + 6], xh).then_inc(s["first_stats"], 1)
            dve.wait_ge(s["padded_ready"], IMAGES + 2)
            group_norm_terms(1, 4 * IMAGES)

            dve.wait_ge(s["table_in"], 32)
            for i in range(2):
                parts = [tparts[i][:, HEADS * k:HEADS * k + HEADS] for k in range(3)]
                link(nc.vector.tensor_copy(parts[0], table[i]))
                link(nc.vector.tensor_tensor(trest[i], table[i], parts[0], ALU.subtract))
                link(nc.vector.tensor_copy(parts[1], trest[i]))
                nc.vector.tensor_tensor(parts[2], trest[i], parts[1], ALU.subtract).then_inc(s["table_split"], 1)
            for k, (a, n, at, count) in enumerate(KINDS):
                dve.wait_ge(s["table_picked"], k + 1)
                banks = PS[:, 4 * (k % 2):4 * (k % 2) + 4, :]
                to = bias[:, at:at + HEADS * PATCH * count].rearrange("p (h q t) -> p q t h", h=HEADS, q=PATCH)
                mask = seen[:, at // HEADS:at // HEADS + PATCH * count].rearrange("p (q t) -> p q t", q=PATCH)
                for part in range(3):
                    for r in range(2):
                        picked = banks[:, :, 48 * count * r:48 * count * (r + 1)].rearrange(
                            "p b (t k h) -> p b t k h", k=3, h=HEADS)[:, :, :, part, :]
                        other = (mask[:, 4 * r:4 * r + 4, :].unsqueeze(3).broadcast_to([128, 4, count, HEADS]) if part == 0
                                 else to[:, 4 * r:4 * r + 4])
                        last = nc.vector.tensor_tensor(to[:, 4 * r:4 * r + 4], picked, other, ALU.add)
                        if part < 2:
                            dve_steps[0] += 1
                            last.then_inc(s["dve_chain"], 1)
                        elif r:
                            last.then_inc(s["table_kept"], 1)
                    if part < 2:
                        dve.wait_ge(s["dve_chain"], dve_steps[0])
            dve.wait_ge(s["table_kept"], len(KINDS))

            def place_patches(k):
                r, (a, j, col) = PATCH_SOURCES[k]
                dve.wait_ge(s["turned"], k + 1)
                src = turned_bias(k).rearrange("p (r c) -> p r c", c=OUTER_W)[:, :, col:col + MIDDLE_W]
                slots = [(b, i) for b in range(2) for i in range(BIAS_PATCHES) if patch_source(b, i) == (r, (a, j, col))]
                for b, i in slots:
                    last = nc.vector.tensor_copy(biasp[:, b, i, :].rearrange("p (r c) -> p r c", c=MIDDLE_W), src)
                last.then_inc(s["placed"], 1)

            for k, (r, (a, j0, _)) in enumerate(PATCH_SOURCES):
                if k >= 8:
                    dve.wait_ge(s["turned"], k - 7)
                at = bias_at(a, OUTER_KINDS[r])
                nc.vector.tensor_copy(biasb[k % 8], bias[:, at:at + HEADS * PATCH * 3].rearrange(
                    "p (q t) -> p q t", t=3)[:, :, j0]).then_inc(s["rounded"], 1)
                if k >= 2:
                    place_patches(k - 2)
            for k in range(len(PATCH_SOURCES) - 2, len(PATCH_SOURCES)):
                place_patches(k)
            dve.wait_ge(s["placed"], len(PATCH_SOURCES))
            nc.vector.memset(small[:, 2, 0:1], 0.0).then_inc(s["init"], 1)
            dve.wait_ge(s["init"], INITS)

            def next_image(j, i, img):
                if i:
                    wait(dve, "misc_in", misc_qkv(i - 1, 2, 1) + 1, j)
                normalize(xn[:, :].rearrange("p (r c) -> p r c", c=SIDE), img, "xn_ready")

            def spread(j, c, heads):
                a = c % 2
                if heads[0] == 0 and a == 0:
                    wait(dve, "misc_out", misc_qkv(c // 2, 0, 1) + 1, j)
                for h in heads:
                    last = nc.vector.tensor_scalar(Qbd[a][:, h, :, :], qs[:, a, :, :], cst[:, C_HEAD + h:C_HEAD + h + 1],
                                                   None, ALU.mult)
                if heads[-1] == HEADS - 1:
                    last.then_inc(s["qbd"], 1)

            def maxima(j, c, b):
                first, count, _ = patch_bank(c % 2, b)
                wait(dve, "peak_in", CHUNK_BANKS * c + b + 1, j)
                if b == 0 and c:
                    wait(dve, "mrow", 16 * c, j)
                nc.vector.tensor_reduce(out=mcol[:, first:first + count],
                                        in_=PS[:, PEAK, 0:PATCH_KEYS * count].rearrange("p (t k) -> p t k", k=PATCH_KEYS),
                                        axis=AX.X, op=ALU.max).then_inc(s["peak_out"], 1)

            def add_bias(j, c, n):
                cols = HEADS * PATCH * tile_of(c % 2, n)[1]
                T = TILES * c + n
                wait(dve, "scores", T + 1, j)
                wait(dve, "weighted", T - 3, j)
                at = bias_at(c % 2, n)
                nc.vector.tensor_tensor(S[:, n % 4, 0:cols], PS[:, SCORE + n % 2, 0:cols], bias[:, at:at + cols], ALU.add
                                        ).then_inc(s["biased"], 1)

            def select_heads(j, c, n):
                q = PATCH * tile_of(c % 2, n)[1]
                T = TILES * c + n
                wait(dve, "weighted", T + 1, j)
                wait(dve, "half", T - 1, j)
                src = PS[:, SUM + n % 2, 0:8 * q].rearrange("p (g h q) -> p g h q", g=2, h=4)
                mask = cst[:, C_OUT:C_OUT + 4].unsqueeze(1).unsqueeze(3).broadcast_to([128, 2, 4, q])
                nc.vector.tensor_tensor(masked[:, n % 2, 0:8 * q].rearrange("p (g h q) -> p g h q", g=2, h=4), src, mask,
                                        ALU.mult).then_inc(s["selected"], 1)

            def divide(j, c):
                wait(dve, "den_in", 32 * (c + 1), j)
                nc.vector.reciprocal(den[:, :], den[:, :]).then_inc(s["recip"], 1)
                wait(dve, "recip", c + 1, j)
                wait(dve, "misc_in", misc_project(c - 1) + 1, j)
                nc.vector.tensor_tensor(normed[:, :], sel[:, (c + 1) % 2, :, :, :].rearrange("p g q t -> p (g q t)"),
                                        den[:, :], ALU.mult).then_inc(s["normed"], 1)

            next_image(None, 0, 0)
            spread(None, 0, range(HEADS))
            for b in range(CHUNK_BANKS):
                maxima(None, 0, b)
            add_bias(None, 0, 0)
            with nc.vector.Fori(0, IMAGES // 2) as j:
                for c in range(4):
                    for n in range(TILES):
                        add_bias(j, *((c, n + 1) if n + 1 < TILES else (c + 1, 0)))
                        if n in SPREAD:
                            spread(j, c + 1, SPREAD[n])
                        if FIRST_BANK <= n < FIRST_BANK + CHUNK_BANKS:
                            maxima(j, c + 1, n - FIRST_BANK)
                        if c % 2 == 0 and n == NEXT_IMAGE:
                            next_image(j, c // 2 + 1, (2 * j + c // 2 + 1) % IMAGES)
                        if n == NORMALIZE:
                            divide(j, c)
                        select_heads(j, c, n)
            divide(None, 2 * IMAGES)

        @block.tensor
        def _(pe):
            mm = nc.tensor.matmul
            pe.wait_ge(s["const_in"], 16)
            with nc.tensor.Fori(0, IMAGES // 2) as j:
                for b in range(2):
                    pe.wait_ge(s[f"xin_in{b}"], j * 16 + 16)
                    wait(pe, "xin_kept", b - 1, j, 2)
                    for k in range(PIECES):
                        o = PS[:, 2 * b + k // 4, PIECE * (k % 4):PIECE * (k % 4) + PIECE]
                        last = nc.tensor.transpose(o, xin[b][:, k, :], cst[0:PIECE, C_ID:C_ID + PIECE])
                    last.then_inc(s["xin_turned"], 1)

            def group_sums(k):
                pe.wait_ge(s["mean_in"], k + 1)
                mm(PS[:, PEAK, 0:IMAGES], group, mv[:, :, 0], start=True, stop=True).then_inc(s["mean_sum"], 1)
                pe.wait_ge(s["var_in"], k + 1)
                mm(PS[:, PEAK, 0:IMAGES], group, small[:, 2, :], start=True, stop=True).then_inc(s["var_sum"], 1)

            group_sums(0)
            with nc.tensor.Fori(0, IMAGES // 2) as j:
                for b in range(2):
                    pe.wait_ge(s["padded_ready"], j * 2 + b + 1)
                    image = padded[b].rearrange("p (r c) -> p r c", c=PAD)
                    for half in range(2):
                        wait(pe, "conv_added", 2 * b + half - 3, j, 4)
                        for tap in range(9):
                            r, c = tap // 3 + HALF_ROWS * half, tap % 3
                            last = mm(PS[:, 2 * b + half, 0:HALF], wconv[:, tap, :], image[:, r:r + HALF_ROWS, c:c + SIDE],
                                      start=tap == 0, stop=tap == 8)
                        last.then_inc(s["conv"], 1)
            group_sums(1)

            pe.wait_ge(s["table_split"], 2)
            for k, (a, n, at, count) in enumerate(KINDS):
                if k < 2:
                    wait(pe, "conv_added", 2 * IMAGES)
                    pe.wait_ge(s["sqrt_in"], 2)
                else:
                    pe.wait_ge(s["table_kept"], k - 1)
                for bank in range(4):
                    for r in range(2):
                        for j in range(count):
                            o = PS[:, 4 * (k % 2) + bank, 48 * (r * count + j):48 * (r * count + j) + 48]
                            first = selection_at(a, n, 4 * r + bank, j)
                            for i in range(2):
                                last = mm(o, chosen[i][0:TABLE_PARTS[i], first:first + 128], tparts[i],
                                          start=i == 0, stop=i == 1)
                last.then_inc(s["table_picked"], 1)
            pe.wait_ge(s["table_kept"], len(KINDS))
            for k in range(len(PATCH_SOURCES)):
                pe.wait_ge(s["rounded"], k + 1)
                if k >= 8:
                    pe.wait_ge(s["placed"], k - 7)
                nc.tensor.transpose(turned_bias(k), biasb[k % 8], identb[:, :]).then_inc(s["turned"], 1)

            def project_qkv(j, i, which, half):
                k = misc_qkv(i, which, half)
                if which == half == 0:
                    wait(pe, "xn_ready", i + 1, j)
                if k:
                    wait(pe, "misc_out", k, j)
                mm(PS[:, MISC, 0:HALF], wqkv[:, CH * which:CH * which + CH], xn[:, HALF * half:HALF * half + HALF],
                   start=True, stop=True).then_inc(s["misc_in"], 1)

            def turn_values(j, c, n, w):
                if n == 0 and c % 2 == 0:
                    wait(pe, "misc_out", misc_qkv(c // 2, 2, 1) + 1, j)
                if w:
                    wait(pe, "value_out", w - 1, j)
                key = tile_of(c % 2, n)[2]
                nc.tensor.transpose(PS[:, VALUE + w % 2, 0:128], V[c // 2 % 2][:, key:key + 128], ident
                                    ).then_inc(s["value_in"], 1)

            def score_tile(j, c, n):
                a, T = c % 2, TILES * c + n
                t0, count, key, _ = tile_of(a, n)
                if n == 0:
                    wait(pe, "mrow", 16 * (c + 1), j)
                if T > 1:
                    wait(pe, "biased", T - 1, j)
                o = PS[:, SCORE + n % 2, 0:HEADS * PATCH * count]
                mm(o, K[c // 2 % 2][:, key:key + 128], Qbd[a][:, :, :, t0:t0 + count], start=True, stop=False)
                row = slice(32 * a, 32 * a + 1)
                mm(o, minus[row, :], mrow[row, :].rearrange("o (p t) -> o p t", p=128)[:, :, t0:t0 + count],
                   start=False, stop=True).then_inc(s["scores"], 1)

            def patch_scores(j, c, b):
                a = c % 2
                first, count, table_first = patch_bank(a, b)
                if b == 0:
                    wait(pe, "qbd", c + 1, j)
                    if a == 0:
                        wait(pe, "misc_out", misc_qkv(c // 2, 1, 1) + 1, j)
                wait(pe, "peak_out", CHUNK_BANKS * c + b, j)
                mm(PS[:, PEAK, 0:PATCH_KEYS * count], identb[:, :], biasp[:, a, table_first:table_first + count, :],
                   start=True, stop=False)
                queries = Qbd[a][:, :, :, :].rearrange("p h q t -> p (h q t)").bitcast(BF16).rearrange(
                    "p (q t two) -> p q t two", q=128, two=2)
                keys = K[c // 2 % 2][:, :].bitcast(BF16).rearrange("p (k two) -> p k two", two=2)[:, :, 1]
                for i in range(count):
                    key, width = patch_keys(a, first + i)
                    window = keys[:, key - key % width:key - key % width + 8 * width].rearrange("p (r c) -> p r c", c=width)
                    window = window[:, :, key % width:key % width + MIDDLE_W]
                    last = mm(PS[:, PEAK, PATCH_KEYS * i:PATCH_KEYS * (i + 1)], queries[:, :, first + i, 1], window,
                              start=False, stop=i == count - 1)
                last.then_inc(s["peak_in"], 1)

            def weigh(j, c, n):
                T = TILES * c + n
                _, count, _, w = tile_of(c % 2, n)
                w += WINDOWS * c
                q = 4 * PATCH * count
                wait(pe, "probs", T + 1, j)
                if new_window(n) is not None:
                    wait(pe, "value_out", w + 1, j)
                wait(pe, "selected", T - 1, j)
                for g in range(4):
                    at = q * (g // 2)
                    last = mm(PS[64 * (g % 2):64 * (g % 2) + 64, SUM + n % 2, at:at + q], VT[:, w % 4, g, :],
                              S[:, n % 4, q * g:q * (g + 1)], start=True, stop=True)
                last.then_inc(s["weighted"], 1)

            def project_out(j, c):
                k = misc_project(c)
                wait(pe, "normed", c + 1, j)
                wait(pe, "misc_out", k, j)
                for g in range(2):
                    last = mm(PS[:, MISC, 0:CHUNK_Q], wproj[:, g, :], normed[:, CHUNK_Q * g:CHUNK_Q * (g + 1)],
                              start=g == 0, stop=g == 1)
                last.then_inc(s["misc_in"], 1)

            def turn_image(j, i, part):
                k = misc_turn(i, part)
                if part == 0:
                    wait(pe, "residual", i + 1, j)
                wait(pe, "misc_out", k, j)
                for p in range(4 - part):
                    at = PIECE * (4 * part + p)
                    last = nc.tensor.transpose(PS[0:PIECE, MISC, CH * p:CH * p + CH], yo[:, at:at + PIECE], ident)
                last.then_inc(s["misc_in"], 1)

            pe.wait_ge(s["init"], INITS)
            pe.wait_ge(s["loaded"], SMALL_LOADS)
            pe.wait_ge(s["pool_loaded"], POOL_LOADS)
            for which in range(3):
                for half in range(2):
                    project_qkv(None, 0, which, half)
            turn_values(None, 0, 0, 0)
            for b in range(CHUNK_BANKS):
                patch_scores(None, 0, b)
            score_tile(None, 0, 0)
            score_tile(None, 0, 1)
            with nc.tensor.Fori(0, IMAGES // 2) as j:
                for c in range(4):
                    for n in range(TILES):
                        score_tile(j, *((c, n + 2) if n + 2 < TILES else (c + 1, n + 2 - TILES)))
                        window = window_for_next(c, n)
                        if window:
                            turn_values(j, *window)
                        if FIRST_BANK <= n < FIRST_BANK + CHUNK_BANKS:
                            patch_scores(j, c + 1, n - FIRST_BANK)
                        if n == MISC_PROJECT:
                            project_out(j, c)
                        if c % 2 == 0 and MISC_QKV <= n < MISC_QKV + 6:
                            project_qkv(j, c // 2 + 1, (n - MISC_QKV) // 2, (n - MISC_QKV) % 2)
                        if c % 2 == 0 and MISC_TURN <= n < MISC_TURN + 2:
                            turn_image(j, c // 2, n - MISC_TURN)
                        weigh(j, c, n)
            project_out(None, 2 * IMAGES)
            for part in range(2):
                turn_image(None, IMAGES, part)


def kernel(x, L0_conv_W, L1_conv_w_qkv, L1_conv_b_qkv, L1_conv_rpb, L1_conv_w_proj, L1_conv_b_proj):
    import numpy as np
    import concourse.bacc as bacc
    from concourse.bass_utils import run_bass_kernel_spmd

    given = {
        "x": np.ascontiguousarray(x).reshape(IMAGES, POS, CH), "conv_w": np.ascontiguousarray(L0_conv_W),
        "w_qkv": np.ascontiguousarray(L1_conv_w_qkv), "b_qkv": np.ascontiguousarray(L1_conv_b_qkv),
        "rpb": np.ascontiguousarray(L1_conv_rpb), "w_proj": np.ascontiguousarray(L1_conv_w_proj),
        "b_proj": np.ascontiguousarray(L1_conv_b_proj),
    }
    given["const"], given["window"], given["select"] = constants()
    nc = bacc.Bacc("TRN2", target_bir_lowering=False, num_devices=1)
    aps = [nc.dram_tensor(n, a.shape, mybir.dt.from_np(a.dtype), kind="ExternalInput").ap() for n, a in given.items()]
    out = nc.dram_tensor("out", (IMAGES, POS, CH), mybir.dt.float32, kind="ExternalOutput").ap()
    build(nc, *aps, out)
    r = run_bass_kernel_spmd(nc, [given], core_ids=[0])
    return r.results[0]["out"].reshape(IMAGES, SIDE, SIDE, CH)
```

```python
from contextlib import ExitStack

import concourse.bass as bass
from concourse import mybir

IMAGES, SIDE, CH = 16, 28, 128
POS = SIDE * SIDE
HEADS, HEAD_DIM = 16, 8
WIN, REACH = 7, 3
TABLE = 2 * WIN - 1
HALF = POS // 2
HALF_ROWS = SIDE // 2
NORM_GROUP = 4
PAD = SIDE + 2
PIECES, PIECE = 7, POS // 7

PATCH = 8
ROWS_OF_PATCHES = SIDE // 2
OUTER_PATCHES = 3 * ROWS_OF_PATCHES
MIDDLE_PATCHES = ROWS_OF_PATCHES // 2
PATCHES = OUTER_PATCHES + MIDDLE_PATCHES
CHUNK_Q = PATCH * PATCHES
TILES = 16

OUTER_W, MIDDLE_W, MIDDLE_COL = 16, 10, 9
OUTER_COL = (0, SIDE - OUTER_W)
STRIP = PAD * OUTER_W
MIDDLE_AT = 2 * STRIP
VALUES = MIDDLE_AT + 320
MIDDLE_FIRST, MIDDLE_ROWS = (0, 12), 19
CHUNK_KEYS = STRIP + 192

PAIRS = ((0, 0), (0, 1), (1, 0), (1, 1), (0, 2), (2, 0))
HEAD_ROWS = len(PAIRS) * HEAD_DIM
PEAK_ROW = 2 * HEAD_ROWS
HEAD_PAIRS = HEADS // 2
WINDOWS = 14

OUTER_KINDS = (0, 1, 2, 12, 13)
NEG = -1.0e30

CHUNK_BANKS = 9
PATCH_KEYS = 80
BIAS_PATCHES = 25


def outer_window(rt):
    return min(max(rt - 1, 0), 11)


def tile_of(a, n):
    if n < ROWS_OF_PATCHES:
        u = outer_window(n)
        return 3 * n, 3, 2 * u * OUTER_W, a * STRIP + 2 * u * OUTER_W, u
    first, count, row = middle_tile(a, n)
    return (first, count, STRIP + (row + 1 - MIDDLE_FIRST[a]) * MIDDLE_W, MIDDLE_AT + (row + 1) * MIDDLE_W, n - 2)


def middle_tile(a, n):
    return {(0, 14): (42, 4, 0), (0, 15): (46, 3, 5), (1, 14): (42, 3, 11), (1, 15): (45, 4, 17)}[a, n]


def bias_kinds(a):
    out, at = [], a * BIAS_COLS // 2
    for n in (*OUTER_KINDS, 14, 15):
        count = tile_of(a, n)[1]
        out.append((n, at, count))
        at += HEADS * PATCH * count
    return out


BIAS_COLS = 2 * HEADS * PATCH * (3 * len(OUTER_KINDS) + MIDDLE_PATCHES)


def bias_at(a, n):
    kind = n if n in (0, 1, 12, 13, 14, 15) else 2
    return next(at for m, at, _ in bias_kinds(a) if m == kind)


def kind_of_row(rt):
    return OUTER_KINDS.index(rt if rt in OUTER_KINDS else 2)


def patch_bank(a, b):
    if b < 7:
        return 6 * b, 6, (0 if b == 0 else 12 if b == 6 else 6)
    n = 14 + b - 7
    first, count, _ = middle_tile(a, n)
    return first, count, 18 + first - OUTER_PATCHES


def patch_keys(a, t):
    if t >= OUTER_PATCHES:
        rt = MIDDLE_PATCHES * a + t - OUTER_PATCHES
        return STRIP + (2 * outer_window(rt) - MIDDLE_FIRST[a]) * MIDDLE_W, 0, MIDDLE_W
    rt, j = divmod(t, 3)
    return 2 * outer_window(rt) * OUTER_W, PATCH_COL[a][j], OUTER_W


PATCH_COL = ((0, 1, 5), (1, 5, 6))

LEFT, WHOLE, RIGHT = (0, 0, 0), (0, 1, 1), (1, 2, 6)
PATCH_SOURCES = [(r, source) for r in range(len(OUTER_KINDS)) for source in (LEFT, WHOLE, RIGHT)]


def patch_source(a, i):
    if i >= 18:
        return kind_of_row(MIDDLE_PATCHES * a + i - 18), WHOLE
    r, j = divmod(i, 3)
    return (0, 1, 2, 2, 3, 4)[r], {(0, 0): LEFT, (1, 2): RIGHT}.get((a, j), WHOLE)


SEL_OUTER = TABLE * OUTER_W
SEL_MIDDLE_FIRST = -4
SEL_MIDDLE = 24 * MIDDLE_W
SEL_COLS = 24 * SEL_OUTER + 4 * SEL_MIDDLE
TABLE_SPLIT = 7
TABLE_PARTS = (TABLE_SPLIT * TABLE, (TABLE - TABLE_SPLIT) * TABLE)


def query_of(a, n, q, j):
    r, c = divmod(q, 4)
    if n < ROWS_OF_PATCHES:
        return 2 * n + r, 16 * a + 4 * j + c
    first = middle_tile(a, n)[0] - OUTER_PATCHES
    return 2 * (MIDDLE_PATCHES * a + first + j) + r, 12 + c


def selection_at(a, n, q, j):
    row, col = query_of(a, n, q, j)
    if n < ROWS_OF_PATCHES:
        first = 2 * outer_window(n) - 1
        return (12 * a + col - 16 * a) * SEL_OUTER + (first - row + WIN - 1) * OUTER_W
    first = middle_tile(a, n)[2]
    return 24 * SEL_OUTER + (col - 12) * SEL_MIDDLE + (first - row + WIN - 1 - SEL_MIDDLE_FIRST) * MIDDLE_W


C_ID, C_GROUP, C_HEAD, C_OUT, CONSTS = 0, 128, 256, 272, 276


BF16_ONE = 0x3F80


def constants():
    import numpy as np

    c = np.zeros((128, CONSTS), np.float32)
    window = np.zeros((128, BIAS_COLS // HEADS), np.float32)
    p = np.arange(128)
    c[:, C_ID:C_ID + 128] = np.eye(128)
    c[:, C_GROUP:C_GROUP + 128] = p[:, None] // NORM_GROUP == p[None] // NORM_GROUP
    c[:, C_HEAD:C_HEAD + HEADS] = (2 * (p % HEAD_PAIRS) + p // 64)[:, None] == np.arange(HEADS)[None]
    c[:, C_OUT:C_OUT + 4] = p[:, None] % 32 // HEAD_DIM == np.arange(4)[None]
    for a in range(2):
        for n, at, count in bias_kinds(a):
            if n < ROWS_OF_PATCHES:
                krow, kcol = 2 * outer_window(n) - 1 + p // OUTER_W, OUTER_COL[a] + p % OUTER_W
            else:
                krow, kcol = middle_tile(a, n)[2] + p // MIDDLE_W, MIDDLE_COL + p % MIDDLE_W
            for q in range(PATCH):
                for j in range(count):
                    row, col = query_of(a, n, q, j)
                    r0, c0 = (min(max(z - REACH, 0), SIDE - WIN) for z in (row, col))
                    seen = (krow >= r0) & (krow < r0 + WIN) & (kcol >= c0) & (kcol < c0 + WIN)
                    window[:, at // HEADS + q * count + j] = np.where(seen, 0.0, NEG)
    sel = np.zeros((2, 128, SEL_COLS), np.float32)
    for dh in range(TABLE):
        for dw in range(TABLE):
            part, entry = (0, dh * TABLE + dw) if dh < TABLE_SPLIT else (1, (dh - TABLE_SPLIT) * TABLE + dw)
            for a in range(2):
                for c12 in range(12):
                    k = dw - (WIN - 1) + 16 * a + c12 - OUTER_COL[a]
                    if 0 <= k < OUTER_W:
                        sel[part, entry, (12 * a + c12) * SEL_OUTER + dh * OUTER_W + k] = 1
            for c4 in range(4):
                k = dw - (WIN - 1) + 12 + c4 - MIDDLE_COL
                if 0 <= k < MIDDLE_W:
                    sel[part, entry, 24 * SEL_OUTER + c4 * SEL_MIDDLE + (dh - SEL_MIDDLE_FIRST) * MIDDLE_W + k] = 1
    return c, window, (sel * BF16_ONE).astype(np.uint16)


def build(nc, x, conv_w, w_qkv, b_qkv, rpb, w_proj, b_proj, const, window, select, out):
    F32, BF16 = mybir.dt.float32, mybir.dt.bfloat16
    ALU, ACT, AX = mybir.AluOpType, mybir.ActivationFunctionType, mybir.AxisListType
    SCALE = float(HEAD_DIM) ** -0.5

    x_mid = nc.dram_tensor("x_mid", (IMAGES, CH, POS), F32, kind="Internal").ap()
    q_parts = nc.dram_tensor("q_parts", (2, 2, len(PAIRS), HEAD_DIM, HEAD_PAIRS, 2 * CHUNK_Q), BF16, kind="Internal").ap()
    k_parts = nc.dram_tensor("k_parts", (2, 2, len(PAIRS), HEAD_DIM, HEAD_PAIRS, 2 * CHUNK_KEYS), BF16, kind="Internal").ap()
    sums = nc.dram_tensor("sums", (2, 8, 2 * CHUNK_Q), F32, kind="Internal").ap()

    ctx = ExitStack()
    with ctx:
        def sb(name, shape, dt=F32):
            return ctx.enter_context(nc.sbuf_tensor(name, shape, dt))

        cst = sb("cst", [128, CONSTS])
        identb = sb("identb", [128, 128], BF16)
        wqkv = sb("wqkv", [128, 3 * CH])
        wqk = sb("wqk", [128, 2, CH])
        bqkv = sb("bqkv", [128, 3])
        wproj = sb("wproj", [128, 2, CH])
        bproj = sb("bproj", [128, 1])
        scratch = sb("scratch", [128, 1])
        mv = sb("mv", [128, IMAGES, 2])
        small = sb("small", [128, 7, IMAGES])
        bias = sb("bias", [128, BIAS_COLS])
        biasp = sb("biasp", [128, 2, BIAS_PATCHES, PATCH_KEYS], BF16)
        S = sb("S", [128, 4, 512])
        VT = sb("VT", [128, 4, 4, 64])
        mcol = sb("mcol", [128, PATCHES], BF16)
        masked = sb("masked", [128, 2, 256])
        halves = sb("halves", [128, 2, 128])
        sel = sb("sel", [128, 2, 2, PATCH, PATCHES])
        packed = sb("packed", [128, PATCHES])
        den = sb("den", [128, 2 * CHUNK_Q])
        normed = sb("normed", [128, 2 * CHUNK_Q])
        xa = sb("xa", [128, POS])
        xn = sb("xn", [128, POS])
        xr = sb("xr", [128, POS])
        yo = sb("yo", [128, POS])
        ot = sb("ot", [PIECE, PIECES, CH])

        area = [sb("area0", [128, IMAGES * POS]), sb("area1", [128, 13032])]

        def part(i, first, size, dt=F32):
            v = area[i][:, first:first + size]
            return v if dt == F32 else v.bitcast(dt)

        X = area[0][:, :].rearrange("p (i n) -> p i n", n=POS)
        wconv = part(1, 0, 9 * CH).rearrange("p (t c) -> p t c", t=9)
        padded = [part(1, 1152 + i * PAD * PAD, PAD * PAD) for i in range(2)]
        xin = [part(1, 2952 + i * 896, 896)[0:PIECE].rearrange("p (k c) -> p k c", k=PIECES) for i in range(2)]
        seen = part(1, 4744, BIAS_COLS // HEADS)
        chosen = [part(1, 5096 + i * SEL_COLS // 2, SEL_COLS // 2, BF16) for i in range(2)]
        stats = yo[:, 0:12 * IMAGES].rearrange("p (i k) -> p i k", k=12)
        table = [sel[0:TABLE_PARTS[i], 0, i, 0, 0:HEADS] for i in range(2)]
        tparts = [masked[0:TABLE_PARTS[i], i, 0:24].bitcast(BF16) for i in range(2)]
        trest = [halves[0:TABLE_PARTS[i], i, 0:HEADS] for i in range(2)]
        biasb = [S[:, 0, 64 * i:64 * i + 64].bitcast(BF16) for i in range(8)]

        KP, QP = HEAD_PAIRS * CHUNK_KEYS // 2, HEAD_PAIRS * CHUNK_Q
        key_rows = [part(0, i * KP, KP, BF16).rearrange("p (g k) -> p g k", g=HEAD_PAIRS) for i in range(2)]
        query_rows = [part(0, 2 * KP + i * QP, QP, BF16).rearrange("p (g h q t) -> p g h q t", g=HEAD_PAIRS, h=2, q=PATCH)
                      for i in range(2)]
        Qbd = part(1, 0, 3136, BF16).rearrange("p (h q t) -> p h q t", h=HEADS, q=PATCH)
        kf = part(1, 3136, 2 * CHUNK_KEYS).rearrange("p (a k) -> p a k", a=2)
        k1 = [part(1, 4480 + i * CHUNK_KEYS, CHUNK_KEYS, BF16) for i in range(2)]
        k23 = [part(1, 5824 + i * CHUNK_KEYS, CHUNK_KEYS, BF16) for i in range(2)]
        rest = part(1, 7168, 2 * CHUNK_KEYS)
        V = [part(1, 8512 + i * VALUES, VALUES) for i in range(2)]
        qf = part(1, 11072, POS)
        qparts = [part(1, 11856 + i * CHUNK_Q, CHUNK_Q, BF16) for i in range(3)]

        KINDS = [(a, n, at, count) for a in range(2) for n, at, count in bias_kinds(a)]

        def turned_bias(k):
            return PS[:, k % 8, 0:64].bitcast(BF16)

        PS = ctx.enter_context(nc.psum_tensor("PS", [128, 8, 512], F32))
        SCORE, SUM, VALUE, PEAK, MISC = 0, 2, 4, 5, 6

        ROWS_IN = 16 * 4

        CREDIT = {"xin_kept": 2, "conv_added": 4, "weighted": 4, "selected": 2, "half": 2,
                  "value_out": 1, "summed": 1, "normed": 1, "out_done": 1}
        EACH = {"misc_in": 20, "misc_out": 20, "rows_in": 4 * ROWS_IN, "middle_in": 64, "scores": 64, "biased": 64, "probs": 64,
                "weighted": 64, "selected": 64, "half": 64, "summed": 64, "qbd": 4, "peak_in": 4 * CHUNK_BANKS,
                "peak_out": 4 * CHUNK_BANKS, "value_in": 4 * WINDOWS, "value_out": 4 * WINDOWS,
                "lead": 6, "rest": 12, "second": 6, "third": 12, "k_stored": 192, "q_stored": 192,
                "sums_out": 128, "packed_in": 64, "recip": 4, "recip_out": 64, "den_in": 128, "normed": 4,
                "xa_in": 32, "xr_in": 32, "residual": 2, "out_done": 32, "xn_ready": 2}
        s = {name: ctx.enter_context(nc.semaphore("s_" + name)) for name in (
            *EACH, "init", "scratch", "warm", "cleared", "x_mid_out", "pool_loaded", "const_in", "loaded", "xin_in0", "xin_in1", "xin_turned", "xin_kept", "table_in", "table_split",
            "table_picked", "table_kept", "rounded", "turned", "placed", "dve_chain", "mean_in", "mean_sum", "var_in",
            "var_sum", "sqrt_in", "sqrt_out", "padded_ready", "conv", "conv_added", "first_stats")}

        def wait(eng, name, k, j=None, each=None):
            k += CREDIT.get(name, 0)
            assert k >= 0 if j is None else k > 0, (name, k)
            eng.wait_ge(s[name], k if j is None else j * (each or EACH[name]) + k)

        ident, group = cst[:, C_ID:C_ID + 128], cst[:, C_GROUP:C_GROUP + 128]
        MEAN, RSTD = 0, 1
        INITS = 18
        SMALL_LOADS, POOL_LOADS = 16 * 5, 16 * (4 + 32 + 2 + 1)
        MISC_IMAGE, MISC_FIRST = 10, 6
        block = ctx.enter_context(nc.Block())

        Q, KEY, VAL = range(3)
        PROJECTED = {0: (KEY, 0), 1: (KEY, 1), 5: (Q, 0), 7: (Q, 1), 20: (VAL, 0), 22: (VAL, 1)}
        MISC_PROJECT, MISC_TURN = 12, 18
        SPREAD = {12: range(0, 2), 13: range(2, 4), 14: range(4, 6), 15: range(6, 8),
                  0: range(8, 11), 1: range(11, 14), 2: range(14, 16)}
        FIRST_BANK, RECIPROCAL, NORMALIZE, NEXT_IMAGE, RESIDUAL = 3, 4, 11, 30, 14
        K_PIECE, Q_PIECE = CHUNK_KEYS // 2, CHUNK_Q
        LEAD = {3: ("k", 0), 4: ("k", 1), 10: ("q", 0)}
        SECOND = {7: ("k", 0), 9: ("k", 1), 14: ("q", 0)}
        REST = {4: ("k", 0), 5: ("k", 1), 6: ("k", 2), 7: ("k", 3), 11: ("q", 0), 12: ("q", 1)}
        THIRD = {8: ("k", 0), 9: ("k", 1), 10: ("k", 2), 13: ("k", 3), 16: ("q", 0), 17: ("q", 1)}

        def misc_project(c):
            return MISC_FIRST + MISC_IMAGE * (c // 2) + (9 if c % 2 else 4 if c < 2 * IMAGES else 0)

        def misc_qkv(i, which, half):
            at = 2 * (KEY, Q, VAL).index(which) + half
            return MISC_IMAGE * (i - 1) + MISC_FIRST + at + (3 if which == VAL else 0) if i else at

        def misc_turn(i, part):
            return MISC_FIRST + MISC_IMAGE * i + (5 if i < IMAGES else 1) + part

        def new_window(n):
            w = tile_of(0, n)[4]
            return w if n == 0 or tile_of(0, n - 1)[4] != w else None

        def window_for_next(c, n):
            c, n = (c, n + 1) if n + 1 < TILES else (c + 1, 0)
            w = new_window(n)
            return None if w is None else (c, n, WINDOWS * c + w)

        def tiles_until(w):
            c, k = divmod(w, WINDOWS)
            return TILES * c + max(n for n in range(TILES) if tile_of(0, n)[4] == k) + 1

        @block.sync
        def _(sp):
            for b in range(2):
                sp.dma_start(xin[b], x[b].rearrange("(k p) c -> p k c", p=PIECE)).then_inc(s[f"xin_in{b}"], 16)
            sp.dma_start(cst[:, :], const).then_inc(s["const_in"], 16)
            sp.dma_start(wqkv[:, :], w_qkv).then_inc(s["loaded"], 16)
            for k in range(3):
                order = "(g l d o) -> l d g o" if k < 2 else "(l d g o) -> l d g o"
                sp.dma_start(bqkv[:, k:k + 1], b_qkv[CH * k:CH * (k + 1)].rearrange(order, l=2, d=HEAD_DIM, o=1),
                             allow_slow_non_contiguous=True).then_inc(s["loaded"], 16)
            sp.dma_start(bproj[:, :], b_proj.rearrange("(p o) -> p o", o=1)).then_inc(s["loaded"], 16)
            with nc.sync.Fori(0, IMAGES // 2 - 1) as j:
                for b in range(2):
                    wait(sp, "xin_turned", b + 1, j, 2)
                    sp.dma_start(xin[b], x[2 * j + 2 + b].rearrange("(k p) c -> p k c", p=PIECE)).then_inc(s[f"xin_in{b}"], 16)

            with nc.sync.Fori(0, IMAGES // 2) as j:
                for b in range(2):
                    wait(sp, "conv_added", 2 * b + 2, j, 4)
                    sp.dma_start(x_mid[2 * j + b], X[:, 2 * j + b, :]).then_inc(s["x_mid_out"], 16)

            def load_next(img):
                sp.dma_start(xa[:, :], x_mid[img]).then_inc(s["xa_in"], 16)

            def load_residual(img):
                sp.dma_start(xr[:, :], x_mid[img]).then_inc(s["xr_in"], 16)

            def store_parts(to, parts, slots, done):
                for slot, part in enumerate(slots):
                    sp.dma_start(to.rearrange("l s d g n -> s l (d g) n")[slot], parts[part]).then_inc(s[done], 16)

            def store_keys(j, i):
                wait(sp, "third", 6 * i + 4, j)
                store_parts(k_parts[i % 2], (k1[i % 2], k23[0], k23[1]), [k for _, k in PAIRS], "k_stored")

            def store_queries(j, i):
                wait(sp, "third", 6 * i + 6, j)
                store_parts(q_parts[i % 2], qparts, [q for q, _ in PAIRS], "q_stored")

            def fill_queries(j, c):
                if c % 2 == 0:
                    wait(sp, "q_stored", 96 * (c // 2 + 1), j)
                for l in range(2):
                    sp.dma_start(query_rows[c % 2][HEAD_ROWS * l:HEAD_ROWS * (l + 1), :, l, :, :].rearrange("r g q t -> r g (q t)"),
                                 q_parts[c // 2 % 2, l].rearrange("s d g (a n) -> a (s d) g n", a=2)[c % 2]
                                 ).then_inc(s["rows_in"], 16)

            def fill_keys(j, c):
                if c % 2 == 0:
                    wait(sp, "k_stored", 96 * (c // 2 + 1), j)
                sp.dma_start(key_rows[c % 2][0:PEAK_ROW],
                             k_parts[c // 2 % 2].rearrange("l s d g (a n) -> a (l s d) g n", a=2)[c % 2]
                             ).then_inc(s["rows_in"], 16)

            def move_maxima(j, c, middle):
                banks, patches = ((CHUNK_BANKS, slice(OUTER_PATCHES, PATCHES)) if middle
                                  else (CHUNK_BANKS - 2, slice(0, OUTER_PATCHES)))
                wait(sp, "peak_out", c * CHUNK_BANKS + banks, j)
                row = query_rows[c % 2][PEAK_ROW:PEAK_ROW + 1].rearrange("o g h q t -> o (g h q) t")
                sp.dma_start(row[:, :, patches], mcol[:, patches]).then_inc(s["middle_in" if middle else "rows_in"], 16)

            def collect_denominators(j, c):
                to = sums[(c + 1) % 2]
                wait(sp, "summed", TILES * c, j)
                for g in range(2):
                    sp.dma_start(to[4 * g:4 * g + 4, :],
                                 sel[64 * g + 32:64 * g + 64:HEAD_DIM, (c + 1) % 2, :, :, :].rearrange("p g q t -> p (g q t)")
                                 ).then_inc(s["sums_out"], 16)
                wait(sp, "sums_out", 32 * (c + 1), j)
                sp.dma_start(packed[:, :], to.rearrange("h n -> (h n)").rearrange("(p n) -> p n", p=128)
                             ).then_inc(s["packed_in"], 16)

            def spread_reciprocals(j, c):
                to = sums[(c + 1) % 2]
                wait(sp, "recip", c + 1, j)
                sp.dma_start(to.rearrange("h n -> (h n)").rearrange("(p n) -> p n", p=128), packed[:, :]
                             ).then_inc(s["recip_out"], 16)
                wait(sp, "recip_out", 16 * (c + 1), j)
                for g in range(2):
                    src = to[4 * g:4 * g + 4, :].unsqueeze(1).broadcast_to([4, HEAD_DIM, 2 * CHUNK_Q])
                    sp.dma_start(den[64 * g:64 * g + 32, :], src).then_inc(s["den_in"], 16)

            def store(j, i, img):
                wait(sp, "misc_out", misc_turn(i, 1) + 1, j)
                sp.dma_start(out[img].rearrange("(k p) c -> p k c", p=PIECE), ot[:, :, :]).then_inc(s["out_done"], 16)

            sp.wait_ge(s["x_mid_out"], 16 * IMAGES)
            sp.wait_ge(s["init"], INITS)
            load_next(0)
            load_residual(IMAGES - 1)
            store_keys(None, 0)
            store_queries(None, 0)
            sp.wait_ge(s["xn_ready"], 1)
            load_next(1)
            fill_queries(None, 0)
            fill_keys(None, 0)
            move_maxima(None, 0, False)
            move_maxima(None, 0, True)
            sp.wait_ge(s["scores"], 1)
            with nc.sync.Fori(0, IMAGES // 2) as j:
                for c in range(4):
                    i = c // 2
                    collect_denominators(j, c)
                    if c % 2 == 0:
                        fill_queries(j, c + 1)
                        spread_reciprocals(j, c)
                        fill_keys(j, c + 1)
                        load_next((2 * j + i + 2) % IMAGES)
                        move_maxima(j, c + 1, False)
                        move_maxima(j, c + 1, True)
                        store_keys(j, i + 1)
                    else:
                        store_queries(j, i + 1)
                        spread_reciprocals(j, c)
                        fill_keys(j, c + 1)
                        fill_queries(j, c + 1)
                        store(j, i, (2 * j + i + IMAGES - 1) % IMAGES)
                        load_residual(2 * j + i)
                        move_maxima(j, c + 1, False)
                        move_maxima(j, c + 1, True)
            collect_denominators(None, 2 * IMAGES)
            spread_reciprocals(None, 2 * IMAGES)
            store(None, IMAGES, IMAGES - 1)
            wait(sp, "out_done", 16 * (IMAGES + 1))

        @block.gpsimd
        def _(pool):
            nc.gpsimd.memset(wproj[:, :, :], 0.0).then_inc(s["cleared"], 1)
            for ap, value in ((padded[0], 0.0), (padded[1], 0.0), (den[:, :], 1.0)):
                nc.gpsimd.memset(ap, value).then_inc(s["cleared"], 1)
            pool.wait_ge(s["cleared"], 1)
            for g in range(4):
                pool.dma_start(wproj[64 * (g % 2):64 * (g % 2) + 32, g // 2, :], w_proj[32 * g:32 * g + 32, :]
                               ).then_inc(s["pool_loaded"], 16)
            for g in range(CH // NORM_GROUP):
                pool.dma_start(wconv[4 * g:4 * g + 4, :, :], conv_w.rearrange("a b j o -> j (a b) o")
                               ).then_inc(s["pool_loaded"], 16)
            for i in range(2):
                pool.dma_start(chosen[i], select[i].bitcast(BF16)).then_inc(s["pool_loaded"], 16)
            pool.dma_start(seen, window).then_inc(s["pool_loaded"], 16)
            for i in range(2):
                first = TABLE_SPLIT * i
                rows = rpb[:, first:first + TABLE_PARTS[i] // TABLE, :]
                pool.dma_start(table[i], rows.rearrange("h a b -> (a b) h"), allow_slow_non_contiguous=True).then_inc(s["table_in"], 16)
            nc.gpsimd.memset(sel[:, 1, :, :, :], 1.0).then_inc(s["init"], 1)
            pool.wait_ge(s["first_stats"], 4 * IMAGES)
            pool.wait_ge(s["padded_ready"], IMAGES + 2)
            pool.wait_ge(s["x_mid_out"], 16 * IMAGES)
            for a in range(2):
                nc.gpsimd.memset(part(0, 2 * KP + a * QP, QP), 0.0).then_inc(s["init"], 1)
            pool.wait_ge(s["table_kept"], len(KINDS))
            for ap in (kf, V[0], V[1]):
                nc.gpsimd.memset(ap, 0.0).then_inc(s["init"], 1)
            pool.wait_ge(s["mean_in"], 2)
            nc.gpsimd.memset(yo[:, :], 0.0).then_inc(s["init"], 1)
            pool.wait_ge(s["init"], INITS)

            def add_heads(j, c, n):
                t0, count = tile_of(c % 2, n)[:2]
                T = TILES * c + n
                q = PATCH * count
                wait(pool, "selected", T + 1, j)
                if n == 0:
                    wait(pool, "normed", c, j)
                m = masked[:, n % 2, 0:8 * q].rearrange("p (g h q) -> p g h q", g=2, h=4)
                h = halves[:, n % 2, 0:4 * q].rearrange("p (g h q) -> p g h q", g=2, h=2)
                nc.gpsimd.tensor_tensor(h, m[:, :, 0:2, :], m[:, :, 2:4, :], ALU.add).then_inc(s["half"], 1)
                wait(pool, "half", T + 1, j)
                h = halves[:, n % 2, 0:4 * q].rearrange("p (g h a t) -> p g h a t", g=2, h=2, a=PATCH)
                nc.gpsimd.tensor_tensor(sel[:, c % 2, :, :, t0:t0 + count], h[:, :, 0], h[:, :, 1], ALU.add
                                        ).then_inc(s["summed"], 1)

            def add_residual(j, i, img):
                wait(pool, "misc_out", misc_project(2 * i) + 1, j)
                wait(pool, "xr_in", 16 * (i + 1), j)
                nc.gpsimd.tensor_tensor(yo[:, :], yo[:, :], xr[:, :], ALU.add).then_inc(s["residual"], 1)

            def subtract_lead(j, i, kind, piece):
                a, h = divmod(piece, 2)
                if kind == "k":
                    wait(pool, "lead", 3 * i + a + 1, j)
                    v, at = kf[:, a, :], slice(K_PIECE * h, K_PIECE * (h + 1))
                    lead = k1[i % 2][:, CHUNK_KEYS * a + at.start:CHUNK_KEYS * a + at.stop]
                else:
                    wait(pool, "lead", 3 * i + 3, j)
                    v, at = qf, slice(Q_PIECE * piece, Q_PIECE * (piece + 1))
                    lead = qparts[0][:, at]
                nc.gpsimd.tensor_tensor(v[:, at], v[:, at], lead, ALU.subtract).then_inc(s["rest"], 1)

            def subtract_second(j, i, kind, piece):
                a, h = divmod(piece, 2)
                if kind == "k":
                    wait(pool, "second", 3 * i + a + 1, j)
                    at = slice(CHUNK_KEYS * a + K_PIECE * h, CHUNK_KEYS * a + K_PIECE * (h + 1))
                    v, second, third = kf[:, a, K_PIECE * h:K_PIECE * (h + 1)], k23[0][:, at], k23[1][:, at]
                else:
                    wait(pool, "second", 3 * i + 3, j)
                    at = slice(Q_PIECE * piece, Q_PIECE * (piece + 1))
                    v, second, third = qf[:, at], qparts[1][:, at], qparts[2][:, at]
                nc.gpsimd.tensor_tensor(third, v, second, ALU.subtract).then_inc(s["third"], 1)

            for step in REST.values():
                subtract_lead(None, 0, *step)
            for step in THIRD.values():
                subtract_second(None, 0, *step)
            with nc.gpsimd.Fori(0, IMAGES // 2) as j:
                for c in range(4):
                    for n in range(TILES):
                        add_heads(j, c, n)
                        step = n + TILES * (c % 2)
                        if step in REST:
                            subtract_lead(j, c // 2 + 1, *REST[step])
                        if step in THIRD:
                            subtract_second(j, c // 2 + 1, *THIRD[step])
                        if step == RESIDUAL:
                            add_residual(j, c // 2, (2 * j + c // 2 + IMAGES - 1) % IMAGES)
            add_residual(None, IMAGES, IMAGES - 1)

        @block.scalar
        def _(act):
            act.wait_ge(s["scratch"], 1)
            nc.scalar.activation(scratch[:, 0:1], scratch[:, 0:1], ACT.Copy).then_inc(s["warm"], 1)
            with nc.scalar.Fori(0, IMAGES // 2) as j:
                for b in range(2):
                    wait(act, "xin_turned", b + 1, j, 2)
                    nc.scalar.activation(X[:, 2 * j + b, 0:448], PS[:, 2 * b, 0:448], ACT.Copy)
                    nc.scalar.activation(X[:, 2 * j + b, 448:784], PS[:, 2 * b + 1, 0:336], ACT.Copy
                                         ).then_inc(s["xin_kept"], 1)
            for k in range(2):
                act.wait_ge(s["sqrt_in"], k + 1)
                nc.scalar.activation(small[:, 4, :], small[:, 3, :], ACT.Sqrt).then_inc(s["sqrt_out"], 1)
            act.wait_ge(s["loaded"], SMALL_LOADS)
            nc.scalar.mul(bqkv[:, 0:1], bqkv[:, 0:1], SCALE).then_inc(s["init"], 1)
            for which in range(2):
                nc.scalar.activation(wqk[:, which, :].rearrange("p (l d g) -> p l d g", l=2, d=HEAD_DIM),
                                     wqkv[:, CH * which:CH * (which + 1)].rearrange("p (g l d) -> p l d g", l=2, d=HEAD_DIM),
                                     ACT.Copy).then_inc(s["init"], 1)

            def misc(j, k):
                wait(act, "misc_in", k + 1, j)
                return PS[:, MISC + k % 2, 0:HALF]

            def keep(dst, src, func, **kw):
                for d, p in zip(dst, src):
                    last = nc.scalar.activation(d, p, func, **kw)
                last.then_inc(s["misc_out"], 1)

            def keep_qkv(j, i, which, half):
                p = misc(j, misc_qkv(i, which, half)).rearrange("p (r c) -> p r c", c=SIDE)
                if which == Q:
                    dst, src = [], []
                    pr = p.rearrange("p (t r) c -> p t r c", r=2)
                    q = qf.rearrange("p (a q t) -> p a q t", a=2, q=PATCH)
                    for r in range(2):
                        for a in range(2):
                            o = q[:, a, 4 * r:4 * r + 4, 21 * half:21 * half + 21]
                            dst.append(o.rearrange("p c (t j) -> p t j c", j=3))
                            src.append(pr[:, :, r, 16 * a:16 * a + 12].rearrange("p t (j c) -> p t j c", j=3))
                        dst.append(q[:, half, 4 * r:4 * r + 4, OUTER_PATCHES:PATCHES].rearrange("p c t -> p t c"))
                        src.append(pr[:, :, r, 12:16])
                    if i and half == 0:
                        wait(act, "third", 6 * i, j)
                    keep(dst, src, ACT.Identity, scale=SCALE, bias=bqkv[:, 0:1])
                    return
                inner = slice(1 + HALF_ROWS * half, 1 + HALF_ROWS * (half + 1))
                all_rows = slice(0, HALF_ROWS)
                dst, src = [], []

                def piece(buf, w, col, to, rows):
                    dst.append(buf.rearrange("p (r c) -> p r c", c=w)[:, to, :])
                    src.append(p[:, rows, col:col + w])

                for a in range(2):
                    buf = kf[:, a, 0:STRIP] if which == KEY else V[i % 2][:, a * STRIP:(a + 1) * STRIP]
                    piece(buf, OUTER_W, OUTER_COL[a], inner, all_rows)
                if which == VAL:
                    piece(V[i % 2][:, MIDDLE_AT:MIDDLE_AT + PAD * MIDDLE_W], MIDDLE_W, MIDDLE_COL, inner, all_rows)
                else:
                    for a in range(2):
                        first = max(inner.start, MIDDLE_FIRST[a])
                        last = min(inner.stop, MIDDLE_FIRST[a] + MIDDLE_ROWS)
                        piece(kf[:, a, STRIP:STRIP + MIDDLE_ROWS * MIDDLE_W], MIDDLE_W, MIDDLE_COL,
                              slice(first - MIDDLE_FIRST[a], last - MIDDLE_FIRST[a]),
                              slice(first - inner.start, last - inner.start))
                    if i and half == 0:
                        wait(act, "third", 6 * i - 2, j)
                keep(dst, src, ACT.Identity, bias=bqkv[:, which:which + 1])

            def keep_lead(j, i, kind, a):
                if kind == "k":
                    wait(act, "misc_out", misc_qkv(i, KEY, 1) + 1, j)
                    dst, src = k1[i % 2][:, CHUNK_KEYS * a:CHUNK_KEYS * (a + 1)], kf[:, a, :]
                else:
                    wait(act, "misc_out", misc_qkv(i, Q, 1) + 1, j)
                    if i:
                        wait(act, "qbd", 2 * i, j)
                    dst, src = qparts[0], qf
                nc.scalar.activation(dst, src, ACT.Copy).then_inc(s["lead"], 1)

            def keep_second(j, i, kind, a):
                if kind == "k":
                    wait(act, "rest", 6 * i + 2 * (a + 1), j)
                    dst, src = k23[0][:, CHUNK_KEYS * a:CHUNK_KEYS * (a + 1)], kf[:, a, :]
                else:
                    wait(act, "rest", 6 * i + 6, j)
                    dst, src = qparts[1], qf
                nc.scalar.activation(dst, src, ACT.Copy).then_inc(s["second"], 1)

            def keep_value(j, w):
                wait(act, "value_in", w + 1, j)
                if j is not None:
                    wait(act, "weighted", tiles_until(w - 4), j)
                nc.scalar.activation(VT[:, w % 4, :, 0:32],
                                     PS[:, VALUE, 0:128].rearrange("p (g c) -> p g c", g=4),
                                     ACT.Copy).then_inc(s["value_out"], 1)

            def exponentials(j, c, n):
                cols = HEADS * PATCH * tile_of(c % 2, n)[1]
                wait(act, "biased", TILES * c + n + 1, j)
                nc.scalar.activation(S[:, n % 4, 0:cols], S[:, n % 4, 0:cols], ACT.Exp).then_inc(s["probs"], 1)

            def keep_projection(j, c):
                a = (c + 1) % 2
                p = misc(j, misc_project(c)).rearrange("p (q t) -> p q t", q=PATCH)
                img = yo[:, :].rearrange("p (t r c) -> p t r c", r=2, c=SIDE)
                dst, src = [], []
                for r in range(2):
                    for half in range(2):
                        dst.append(img[:, 7 * half:7 * half + 7, r, 16 * a:16 * a + 12].rearrange("p t (j c) -> p t j c", j=3))
                        src.append(p[:, 4 * r:4 * r + 4, 21 * half:21 * half + 21].rearrange("p c (t j) -> p t j c", j=3))
                    dst.append(img[:, 7 * a:7 * a + 7, r, 12:16])
                    src.append(p[:, 4 * r:4 * r + 4, OUTER_PATCHES:PATCHES].rearrange("p c t -> p t c"))
                keep(dst, src, ACT.Identity, bias=bproj[:, 0:1])

            def keep_turned(j, i, part):
                k = misc_turn(i, part)
                misc(j, k)
                if part == 0:
                    wait(act, "out_done", 16 * i, j)
                count = 4 - part
                keep([ot[:, 4 * part:4 * part + count, :]],
                     [PS[0:PIECE, MISC + k % 2, 0:CH * count].rearrange("p (k c) -> p k c", c=CH)], ACT.Copy)

            act.wait_ge(s["init"], INITS)
            act.wait_ge(s["warm"], 1)
            nc.scalar.activation(scratch[:, 0:1], scratch[:, 0:1], ACT.Exp)
            for which in (KEY, Q, VAL):
                for half in range(2):
                    keep_qkv(None, 0, which, half)
            for step in LEAD.values():
                keep_lead(None, 0, *step)
            keep_value(None, 0)
            for step in SECOND.values():
                keep_second(None, 0, *step)
            with nc.scalar.Fori(0, IMAGES // 2) as j:
                for c in range(4):
                    for n in range(TILES):
                        exponentials(j, c, n)
                        window = window_for_next(c, n)
                        if window:
                            keep_value(j, window[2])
                        step = n + TILES * (c % 2)
                        if n == MISC_PROJECT + 1:
                            keep_projection(j, c)
                        if step - 1 in PROJECTED:
                            keep_qkv(j, c // 2 + 1, *PROJECTED[step - 1])
                        if MISC_TURN < step <= MISC_TURN + 2:
                            keep_turned(j, c // 2, step - 1 - MISC_TURN)
                        if step in LEAD:
                            keep_lead(j, c // 2 + 1, *LEAD[step])
                        if step in SECOND:
                            keep_second(j, c // 2 + 1, *SECOND[step])
            keep_projection(None, 2 * IMAGES)
            for part in range(2):
                keep_turned(None, IMAGES, part)

        @block.vector
        def _(dve):
            dve_steps = [0]

            def link(ins):
                dve_steps[0] += 1
                ins.then_inc(s["dve_chain"], 1)
                dve.wait_ge(s["dve_chain"], dve_steps[0])

            nc.vector.memset(scratch[:, :], 0.0).then_inc(s["scratch"], 1)
            for w in range(4):
                nc.vector.memset(VT[:, w, :, :], 1.0).then_inc(s["init"], 1)
            for i, (name, credit) in enumerate(CREDIT.items()):
                nc.vector.memset(small[:, 6, i:i + 1], 0.0).then_inc(s[name], credit)
            dve.wait_ge(s["const_in"], 16)
            nc.vector.tensor_copy(identb[:, :], ident).then_inc(s["init"], 1)

            with nc.vector.Fori(0, IMAGES // 2) as j:
                for b in range(2):
                    wait(dve, "xin_kept", b + 1, j, 2)
                    for half in range(2):
                        nc.vector.bn_stats(stats[:, 2 * j + b, 6 * half:6 * half + 6],
                                           X[:, 2 * j + b, HALF * half:HALF * half + HALF]).then_inc(s["first_stats"], 1)

            def group_norm_terms(k, stats_done):
                dve.wait_ge(s["first_stats"], stats_done)
                for i in range(IMAGES):
                    last = nc.vector.bn_aggr(mv[:, i, :], stats[:, i, :].rearrange("p (h k) -> p h k", k=6))
                last.then_inc(s["mean_in"], 1)
                dve.wait_ge(s["mean_sum"], k + 1)
                link(nc.vector.tensor_scalar(small[:, MEAN, :], PS[:, PEAK, 0:IMAGES], 1.0 / NORM_GROUP, None, ALU.mult))
                dve.wait_ge(s["mean_in"], k + 1)
                link(nc.vector.tensor_tensor(small[:, 2, :], mv[:, :, 0], small[:, MEAN, :], ALU.subtract))
                link(nc.vector.tensor_tensor(small[:, 3, :], small[:, 2, :], small[:, 2, :], ALU.mult))
                nc.vector.tensor_tensor(small[:, 2, :], small[:, 3, :], mv[:, :, 1], ALU.add).then_inc(s["var_in"], 1)
                dve.wait_ge(s["var_sum"], k + 1)
                nc.vector.tensor_scalar(small[:, 3, :], PS[:, PEAK, 0:IMAGES], 1.0 / NORM_GROUP, 1e-5, ALU.mult, ALU.add
                                        ).then_inc(s["sqrt_in"], 1)
                dve.wait_ge(s["sqrt_in"], k + 1)
                dve.wait_ge(s["sqrt_out"], k + 1)
                link(nc.vector.reciprocal(small[:, 5, :], small[:, 4, :]))
                link(nc.vector.tensor_tensor(small[:, 6, :], small[:, 5, :], small[:, 5, :], ALU.mult))
                link(nc.vector.tensor_tensor(small[:, 6, :], small[:, 6, :], small[:, 3, :], ALU.mult))
                link(nc.vector.tensor_scalar(small[:, 6, :], small[:, 6, :], -0.5, 1.5, ALU.mult, ALU.add))
                link(nc.vector.tensor_tensor(small[:, RSTD, :], small[:, 5, :], small[:, 6, :], ALU.mult))

            def normalize(dst, src, img, done):
                nc.vector.tensor_scalar(dst, src.rearrange("p (r c) -> p r c", c=SIDE),
                                        small[:, MEAN, :].unsqueeze(2)[:, img, :], small[:, RSTD, :].unsqueeze(2)[:, img, :],
                                        ALU.subtract, ALU.mult).then_inc(s[done], 1)

            group_norm_terms(0, 2 * IMAGES)

            dve.wait_ge(s["cleared"], 4)
            inner = [padded[b].rearrange("p (r c) -> p r c", c=PAD)[:, 1:1 + SIDE, 1:1 + SIDE] for b in range(2)]
            dve.wait_ge(s["pool_loaded"], POOL_LOADS)
            link(nc.vector.tensor_tensor(wconv, wconv, group.unsqueeze(1).broadcast_to([128, 9, CH]), ALU.mult))
            normalize(inner[0], X[:, 0, :], 0, "padded_ready")
            normalize(inner[1], X[:, 1, :], 1, "padded_ready")
            with nc.vector.Fori(0, IMAGES // 2) as j:
                for b in range(2):
                    for half in range(2):
                        wait(dve, "conv", 2 * b + half + 1, j, 4)
                        xh = X[:, 2 * j + b, HALF * half:HALF * half + HALF]
                        nc.vector.tensor_tensor(xh, xh, PS[:, 2 * b + half, 0:HALF], ALU.add).then_inc(s["conv_added"], 1)
                    img = (2 * j + b + 2) % IMAGES
                    normalize(inner[b], X[:, img, :], img, "padded_ready")
                    for half in range(2):
                        wait(dve, "conv_added", 2 * b + half + 1, j, 4)
                        xh = X[:, 2 * j + b, HALF * half:HALF * half + HALF]
                        nc.vector.bn_stats(stats[:, 2 * j + b, 6 * half:6 * half + 6], xh).then_inc(s["first_stats"], 1)
            dve.wait_ge(s["padded_ready"], IMAGES + 2)
            group_norm_terms(1, 4 * IMAGES)

            dve.wait_ge(s["table_in"], 32)
            for i in range(2):
                parts = [tparts[i][:, HEADS * k:HEADS * k + HEADS] for k in range(3)]
                link(nc.vector.tensor_copy(parts[0], table[i]))
                link(nc.vector.tensor_tensor(trest[i], table[i], parts[0], ALU.subtract))
                link(nc.vector.tensor_copy(parts[1], trest[i]))
                nc.vector.tensor_tensor(parts[2], trest[i], parts[1], ALU.subtract).then_inc(s["table_split"], 1)
            for k, (a, n, at, count) in enumerate(KINDS):
                dve.wait_ge(s["table_picked"], k + 1)
                banks = PS[:, 4 * (k % 2):4 * (k % 2) + 4, :]
                to = bias[:, at:at + HEADS * PATCH * count].rearrange("p (h q t) -> p q t h", h=HEADS, q=PATCH)
                mask = seen[:, at // HEADS:at // HEADS + PATCH * count].rearrange("p (q t) -> p q t", q=PATCH)
                for part in range(3):
                    for r in range(2):
                        picked = banks[:, :, 48 * count * r:48 * count * (r + 1)].rearrange(
                            "p b (t k h) -> p b t k h", k=3, h=HEADS)[:, :, :, part, :]
                        other = (mask[:, 4 * r:4 * r + 4, :].unsqueeze(3).broadcast_to([128, 4, count, HEADS]) if part == 0
                                 else to[:, 4 * r:4 * r + 4])
                        last = nc.vector.tensor_tensor(to[:, 4 * r:4 * r + 4], picked, other, ALU.add)
                        if part < 2:
                            dve_steps[0] += 1
                            last.then_inc(s["dve_chain"], 1)
                        elif r:
                            last.then_inc(s["table_kept"], 1)
                    if part < 2:
                        dve.wait_ge(s["dve_chain"], dve_steps[0])
            dve.wait_ge(s["table_kept"], len(KINDS))

            def place_patches(k):
                r, (a, j, col) = PATCH_SOURCES[k]
                dve.wait_ge(s["turned"], k + 1)
                src = turned_bias(k).rearrange("p (r c) -> p r c", c=OUTER_W)[:, :, col:col + MIDDLE_W]
                slots = [(b, i) for b in range(2) for i in range(BIAS_PATCHES) if patch_source(b, i) == (r, (a, j, col))]
                for b, i in slots:
                    last = nc.vector.tensor_copy(biasp[:, b, i, :].rearrange("p (r c) -> p r c", c=MIDDLE_W), src)
                last.then_inc(s["placed"], 1)

            for k, (r, (a, j0, _)) in enumerate(PATCH_SOURCES):
                if k >= 8:
                    dve.wait_ge(s["turned"], k - 7)
                at = bias_at(a, OUTER_KINDS[r])
                nc.vector.tensor_copy(biasb[k % 8], bias[:, at:at + HEADS * PATCH * 3].rearrange(
                    "p (q t) -> p q t", t=3)[:, :, j0]).then_inc(s["rounded"], 1)
                if k >= 2:
                    place_patches(k - 2)
            for k in range(len(PATCH_SOURCES) - 2, len(PATCH_SOURCES)):
                place_patches(k)
            dve.wait_ge(s["placed"], len(PATCH_SOURCES))
            dve.wait_ge(s["x_mid_out"], 16 * IMAGES)
            for a in range(2):
                nc.vector.memset(key_rows[a][PEAK_ROW:PEAK_ROW + 1], -1.0).then_inc(s["init"], 1)
            nc.vector.memset(small[:, 2, 0:1], 0.0).then_inc(s["init"], 1)
            dve.wait_ge(s["init"], INITS)

            def next_image(j, i, img):
                wait(dve, "xa_in", 16 * (i + 1), j)
                if i:
                    wait(dve, "misc_in", misc_qkv(i - 1, VAL, 1) + 1, j)
                normalize(xn[:, :].rearrange("p (r c) -> p r c", c=SIDE), xa[:, :], img, "xn_ready")

            def spread(j, c, heads):
                if heads[0] == 0:
                    if c % 2 == 0:
                        wait(dve, "lead", 3 * (c // 2) + 3, j)
                    if c:
                        wait(dve, "peak_in", CHUNK_BANKS * c, j)
                for h in heads:
                    last = nc.vector.tensor_scalar(Qbd[:, h, :, :], qparts[0].rearrange(
                        "p (a q t) -> p a q t", a=2, q=PATCH)[:, c % 2], cst[:, C_HEAD + h:C_HEAD + h + 1], None, ALU.mult)
                if heads[-1] == HEADS - 1:
                    last.then_inc(s["qbd"], 1)

            def maxima(j, c, b):
                first, count, _ = patch_bank(c % 2, b)
                wait(dve, "peak_in", CHUNK_BANKS * c + b + 1, j)
                if c and b == CHUNK_BANKS - 2:
                    wait(dve, "middle_in", 16 * c, j)
                nc.vector.tensor_reduce(out=mcol[:, first:first + count],
                                        in_=PS[:, PEAK, 0:PATCH_KEYS * count].rearrange("p (t k) -> p t k", k=PATCH_KEYS),
                                        axis=AX.X, op=ALU.max).then_inc(s["peak_out"], 1)

            def add_bias(j, c, n):
                cols = HEADS * PATCH * tile_of(c % 2, n)[1]
                T = TILES * c + n
                wait(dve, "scores", T + 1, j)
                wait(dve, "weighted", T - 3, j)
                at = bias_at(c % 2, n)
                nc.vector.tensor_tensor(S[:, n % 4, 0:cols], PS[:, SCORE + n % 2, 0:cols], bias[:, at:at + cols], ALU.add
                                        ).then_inc(s["biased"], 1)

            def select_heads(j, c, n):
                q = PATCH * tile_of(c % 2, n)[1]
                T = TILES * c + n
                wait(dve, "weighted", T + 1, j)
                wait(dve, "half", T - 1, j)
                src = PS[:, SUM + n % 2, 0:8 * q].rearrange("p (g h q) -> p g h q", g=2, h=4)
                mask = cst[:, C_OUT:C_OUT + 4].unsqueeze(1).unsqueeze(3).broadcast_to([128, 2, 4, q])
                nc.vector.tensor_tensor(masked[:, n % 2, 0:8 * q].rearrange("p (g h q) -> p g h q", g=2, h=4), src, mask,
                                        ALU.mult).then_inc(s["selected"], 1)

            def invert(j, c):
                wait(dve, "packed_in", 16 * (c + 1), j)
                nc.vector.reciprocal(packed[:, :], packed[:, :]).then_inc(s["recip"], 1)

            def divide(j, c):
                wait(dve, "den_in", 32 * (c + 1), j)
                wait(dve, "misc_in", misc_project(c - 1) + 1, j)
                nc.vector.tensor_tensor(normed[:, :], sel[:, (c + 1) % 2, :, :, :].rearrange("p g q t -> p (g q t)"),
                                        den[:, :], ALU.mult).then_inc(s["normed"], 1)

            next_image(None, 0, 0)
            spread(None, 0, range(HEADS))
            for b in range(CHUNK_BANKS):
                maxima(None, 0, b)
            next_image(None, 1, 1)
            for n in range(12, 16):
                spread(None, 1, SPREAD[n])
            add_bias(None, 0, 0)
            with nc.vector.Fori(0, IMAGES // 2) as j:
                for c in range(4):
                    for n in range(TILES):
                        add_bias(j, *((c, n + 1) if n + 1 < TILES else (c + 1, 0)))
                        if n:
                            select_heads(j, c, n - 1)
                        elif c:
                            select_heads(j, c - 1, TILES - 1)
                        if n in SPREAD:
                            spread(j, c + 2 if n >= 12 else c + 1, SPREAD[n])
                        if FIRST_BANK <= n < FIRST_BANK + CHUNK_BANKS:
                            maxima(j, c + 1, n - FIRST_BANK)
                        if n + TILES * (c % 2) == NEXT_IMAGE:
                            next_image(j, c // 2 + 2, (2 * j + c // 2 + 2) % IMAGES)
                        if n == RECIPROCAL:
                            invert(j, c)
                        if n == NORMALIZE:
                            divide(j, c)
                        if c == 3 and n == TILES - 1:
                            select_heads(j, c, n)
            invert(None, 2 * IMAGES)
            divide(None, 2 * IMAGES)

        @block.tensor
        def _(pe):
            mm = nc.tensor.matmul
            pe.wait_ge(s["const_in"], 16)
            with nc.tensor.Fori(0, IMAGES // 2) as j:
                for b in range(2):
                    pe.wait_ge(s[f"xin_in{b}"], j * 16 + 16)
                    wait(pe, "xin_kept", b - 1, j, 2)
                    for k in range(PIECES):
                        o = PS[:, 2 * b + k // 4, PIECE * (k % 4):PIECE * (k % 4) + PIECE]
                        last = nc.tensor.transpose(o, xin[b][:, k, :], cst[0:PIECE, C_ID:C_ID + PIECE])
                    last.then_inc(s["xin_turned"], 1)

            def group_sums(k):
                pe.wait_ge(s["mean_in"], k + 1)
                mm(PS[:, PEAK, 0:IMAGES], group, mv[:, :, 0], start=True, stop=True).then_inc(s["mean_sum"], 1)
                pe.wait_ge(s["var_in"], k + 1)
                mm(PS[:, PEAK, 0:IMAGES], group, small[:, 2, :], start=True, stop=True).then_inc(s["var_sum"], 1)

            group_sums(0)
            with nc.tensor.Fori(0, IMAGES // 2) as j:
                for b in range(2):
                    pe.wait_ge(s["padded_ready"], j * 2 + b + 1)
                    image = padded[b].rearrange("p (r c) -> p r c", c=PAD)
                    for half in range(2):
                        wait(pe, "conv_added", 2 * b + half - 3, j, 4)
                        for tap in range(9):
                            r, c = tap // 3 + HALF_ROWS * half, tap % 3
                            last = mm(PS[:, 2 * b + half, 0:HALF], wconv[:, tap, :], image[:, r:r + HALF_ROWS, c:c + SIDE],
                                      start=tap == 0, stop=tap == 8)
                        last.then_inc(s["conv"], 1)
            group_sums(1)

            pe.wait_ge(s["table_split"], 2)
            for k, (a, n, at, count) in enumerate(KINDS):
                if k < 2:
                    wait(pe, "conv_added", 2 * IMAGES)
                    pe.wait_ge(s["sqrt_in"], 2)
                else:
                    pe.wait_ge(s["table_kept"], k - 1)
                for bank in range(4):
                    for r in range(2):
                        for j in range(count):
                            o = PS[:, 4 * (k % 2) + bank, 48 * (r * count + j):48 * (r * count + j) + 48]
                            first = selection_at(a, n, 4 * r + bank, j)
                            for i in range(2):
                                last = mm(o, chosen[i][0:TABLE_PARTS[i], first:first + 128], tparts[i],
                                          start=i == 0, stop=i == 1)
                last.then_inc(s["table_picked"], 1)
            pe.wait_ge(s["table_kept"], len(KINDS))
            for k in range(len(PATCH_SOURCES)):
                pe.wait_ge(s["rounded"], k + 1)
                if k >= 8:
                    pe.wait_ge(s["placed"], k - 7)
                nc.tensor.transpose(turned_bias(k), biasb[k % 8], identb[:, :]).then_inc(s["turned"], 1)

            def project_qkv(j, i, which, half):
                k = misc_qkv(i, which, half)
                if which == KEY and half == 0:
                    wait(pe, "xn_ready", i + 1, j)
                if k > 1:
                    wait(pe, "misc_out", k - 1, j)
                weights = wqk[:, which, :] if which < VAL else wqkv[:, CH * VAL:CH * (VAL + 1)]
                mm(PS[:, MISC + k % 2, 0:HALF], weights, xn[:, HALF * half:HALF * half + HALF],
                   start=True, stop=True).then_inc(s["misc_in"], 1)

            def turn_values(j, c, n, w):
                if n == 0 and c % 2 == 0:
                    wait(pe, "misc_out", misc_qkv(c // 2, VAL, 1) + 1, j)
                if w:
                    wait(pe, "value_out", w, j)
                key = tile_of(c % 2, n)[3]
                nc.tensor.transpose(PS[:, VALUE, 0:128], V[c // 2 % 2][:, key:key + 128], ident
                                    ).then_inc(s["value_in"], 1)

            def score_tile(j, c, n):
                a, T = c % 2, TILES * c + n
                t0, count, key = tile_of(a, n)[:3]
                if n == 0:
                    wait(pe, "rows_in", ROWS_IN * (c + 1), j)
                if n == 2:
                    wait(pe, "middle_in", 16 * (c + 1), j)
                if T > 1:
                    wait(pe, "biased", T - 1, j)
                cols = 2 * PATCH * count
                for g in range(HEAD_PAIRS):
                    last = mm(PS[:, SCORE + n % 2, cols * g:cols * (g + 1)], key_rows[a][0:PEAK_ROW + 1, g, key:key + 128],
                              query_rows[a][0:PEAK_ROW + 1, g, :, :, t0:t0 + count], start=True, stop=True)
                last.then_inc(s["scores"], 1)

            def patch_scores(j, c, b):
                a = c % 2
                first, count, table_first = patch_bank(a, b)
                if b == 0:
                    wait(pe, "qbd", c + 1, j)
                    if a == 0:
                        wait(pe, "lead", 3 * (c // 2) + 2, j)
                wait(pe, "peak_out", CHUNK_BANKS * c + b, j)
                mm(PS[:, PEAK, 0:PATCH_KEYS * count], identb[:, :], biasp[:, a, table_first:table_first + count, :],
                   start=True, stop=False)
                queries = Qbd.rearrange("p h q t -> p (h q) t")
                keys = k1[c // 2 % 2][:, CHUNK_KEYS * a:CHUNK_KEYS * (a + 1)]
                for i in range(count):
                    key, col, width = patch_keys(a, first + i)
                    rows = keys[:, key:key + 8 * width].rearrange("p (r c) -> p r c", c=width)
                    last = mm(PS[:, PEAK, PATCH_KEYS * i:PATCH_KEYS * (i + 1)], queries[:, :, first + i],
                              rows[:, :, col:col + MIDDLE_W], start=False, stop=i == count - 1)
                last.then_inc(s["peak_in"], 1)

            def weigh(j, c, n):
                T = TILES * c + n
                _, count, _, _, w = tile_of(c % 2, n)
                w += WINDOWS * c
                q = 4 * PATCH * count
                wait(pe, "probs", T + 1, j)
                if new_window(n) is not None:
                    wait(pe, "value_out", w + 1, j)
                wait(pe, "selected", T - 1, j)
                for g in range(4):
                    at = q * (g // 2)
                    last = mm(PS[64 * (g % 2):64 * (g % 2) + 64, SUM + n % 2, at:at + q], VT[:, w % 4, g, :],
                              S[:, n % 4, q * g:q * (g + 1)], start=True, stop=True)
                last.then_inc(s["weighted"], 1)

            def project_out(j, c):
                k = misc_project(c)
                wait(pe, "normed", c + 1, j)
                wait(pe, "misc_out", k - 1, j)
                for g in range(2):
                    last = mm(PS[:, MISC + k % 2, 0:CHUNK_Q], wproj[:, g, :], normed[:, CHUNK_Q * g:CHUNK_Q * (g + 1)],
                              start=g == 0, stop=g == 1)
                last.then_inc(s["misc_in"], 1)

            def turn_image(j, i, part):
                k = misc_turn(i, part)
                if part == 0:
                    wait(pe, "residual", i + 1, j)
                wait(pe, "misc_out", k - 1, j)
                for p in range(4 - part):
                    at = PIECE * (4 * part + p)
                    last = nc.tensor.transpose(PS[0:PIECE, MISC + k % 2, CH * p:CH * p + CH], yo[:, at:at + PIECE], ident)
                last.then_inc(s["misc_in"], 1)

            pe.wait_ge(s["init"], INITS)
            pe.wait_ge(s["cleared"], 4)
            pe.wait_ge(s["loaded"], SMALL_LOADS)
            pe.wait_ge(s["pool_loaded"], POOL_LOADS)
            for which in (KEY, Q, VAL):
                for half in range(2):
                    project_qkv(None, 0, which, half)
            turn_values(None, 0, 0, 0)
            for b in range(CHUNK_BANKS):
                patch_scores(None, 0, b)
            score_tile(None, 0, 0)
            score_tile(None, 0, 1)
            with nc.tensor.Fori(0, IMAGES // 2) as j:
                for c in range(4):
                    for n in range(TILES):
                        score_tile(j, *((c, n + 2) if n + 2 < TILES else (c + 1, n + 2 - TILES)))
                        window = window_for_next(c, n)
                        if window:
                            turn_values(j, *window)
                        if FIRST_BANK <= n < FIRST_BANK + CHUNK_BANKS:
                            patch_scores(j, c + 1, n - FIRST_BANK)
                        if n == MISC_PROJECT:
                            project_out(j, c)
                        step = n + TILES * (c % 2)
                        if step in PROJECTED:
                            project_qkv(j, c // 2 + 1, *PROJECTED[step])
                        if MISC_TURN <= step < MISC_TURN + 2:
                            turn_image(j, c // 2, step - MISC_TURN)
                        weigh(j, c, n)
            project_out(None, 2 * IMAGES)
            for part in range(2):
                turn_image(None, IMAGES, part)


def kernel(x, L0_conv_W, L1_conv_w_qkv, L1_conv_b_qkv, L1_conv_rpb, L1_conv_w_proj, L1_conv_b_proj):
    import numpy as np
    import concourse.bacc as bacc
    from concourse.bass_utils import run_bass_kernel_spmd

    given = {
        "x": np.ascontiguousarray(x).reshape(IMAGES, POS, CH), "conv_w": np.ascontiguousarray(L0_conv_W),
        "w_qkv": np.ascontiguousarray(L1_conv_w_qkv), "b_qkv": np.ascontiguousarray(L1_conv_b_qkv),
        "rpb": np.ascontiguousarray(L1_conv_rpb), "w_proj": np.ascontiguousarray(L1_conv_w_proj),
        "b_proj": np.ascontiguousarray(L1_conv_b_proj),
    }
    given["const"], given["window"], given["select"] = constants()
    nc = bacc.Bacc("TRN2", target_bir_lowering=False, num_devices=1)
    aps = [nc.dram_tensor(n, a.shape, mybir.dt.from_np(a.dtype), kind="ExternalInput").ap() for n, a in given.items()]
    out = nc.dram_tensor("out", (IMAGES, POS, CH), mybir.dt.float32, kind="ExternalOutput").ap()
    build(nc, *aps, out)
    r = run_bass_kernel_spmd(nc, [given], core_ids=[0])
    return r.results[0]["out"].reshape(IMAGES, SIDE, SIDE, CH)
```

```python
from contextlib import ExitStack

import concourse.bass as bass
from concourse import mybir

IMAGES, SIDE, CH = 16, 28, 128
POS = SIDE * SIDE
HEADS, HEAD_DIM = 16, 8
WIN, REACH = 7, 3
TABLE = 2 * WIN - 1
HALF = POS // 2
HALF_ROWS = SIDE // 2
NORM_GROUP = 4
PAD = SIDE + 2
PIECES, PIECE = 7, POS // 7

PATCH = 8
ROWS_OF_PATCHES = SIDE // 2
OUTER_PATCHES = 3 * ROWS_OF_PATCHES
MIDDLE_PATCHES = ROWS_OF_PATCHES // 2
PATCHES = OUTER_PATCHES + MIDDLE_PATCHES
CHUNK_Q = PATCH * PATCHES
TILES = 16

OUTER_W, MIDDLE_W, MIDDLE_COL = 16, 10, 9
OUTER_COL = (0, SIDE - OUTER_W)
STRIP = PAD * OUTER_W
MIDDLE_AT = 2 * STRIP
VALUES = MIDDLE_AT + 320
MIDDLE_FIRST, MIDDLE_ROWS = (0, 12), 19
CHUNK_KEYS = STRIP + 192

PAIRS = ((0, 0), (0, 1), (1, 0), (1, 1), (0, 2), (2, 0))
HEAD_ROWS = len(PAIRS) * HEAD_DIM
PEAK_ROW = 2 * HEAD_ROWS
HEAD_PAIRS = HEADS // 2
WINDOWS = 14

X_RING = 4
OUTER_KINDS = (0, 1, 2, 12, 13)
NEG = -1.0e30

CHUNK_BANKS = 9
PATCH_KEYS = 80
BIAS_PATCHES = 25


def outer_window(rt):
    return min(max(rt - 1, 0), 11)


def tile_of(a, n):
    if n < ROWS_OF_PATCHES:
        u = outer_window(n)
        return 3 * n, 3, 2 * u * OUTER_W, a * STRIP + 2 * u * OUTER_W, u
    first, count, row = middle_tile(a, n)
    return (first, count, STRIP + (row + 1 - MIDDLE_FIRST[a]) * MIDDLE_W, MIDDLE_AT + (row + 1) * MIDDLE_W, n - 2)


def middle_tile(a, n):
    return {(0, 14): (42, 4, 0), (0, 15): (46, 3, 5), (1, 14): (42, 3, 11), (1, 15): (45, 4, 17)}[a, n]


def bias_kinds(a):
    out, at = [], a * BIAS_COLS // 2
    for n in (*OUTER_KINDS, 14, 15):
        count = tile_of(a, n)[1]
        out.append((n, at, count))
        at += HEADS * PATCH * count
    return out


BIAS_COLS = 2 * HEADS * PATCH * (3 * len(OUTER_KINDS) + MIDDLE_PATCHES)


def bias_at(a, n):
    kind = n if n in (0, 1, 12, 13, 14, 15) else 2
    return next(at for m, at, _ in bias_kinds(a) if m == kind)


def kind_of_row(rt):
    return OUTER_KINDS.index(rt if rt in OUTER_KINDS else 2)


def patch_bank(a, b):
    if b < 7:
        return 6 * b, 6, (0 if b == 0 else 12 if b == 6 else 6)
    n = 14 + b - 7
    first, count, _ = middle_tile(a, n)
    return first, count, 18 + first - OUTER_PATCHES


def patch_keys(a, t):
    if t >= OUTER_PATCHES:
        rt = MIDDLE_PATCHES * a + t - OUTER_PATCHES
        return STRIP + (2 * outer_window(rt) - MIDDLE_FIRST[a]) * MIDDLE_W, 0, MIDDLE_W
    rt, j = divmod(t, 3)
    return 2 * outer_window(rt) * OUTER_W, PATCH_COL[a][j], OUTER_W


PATCH_COL = ((0, 1, 5), (1, 5, 6))

LEFT, WHOLE, RIGHT = (0, 0, 0), (0, 1, 1), (1, 2, 6)
PATCH_SOURCES = [(r, source) for r in range(len(OUTER_KINDS)) for source in (LEFT, WHOLE, RIGHT)]


def patch_source(a, i):
    if i >= 18:
        return kind_of_row(MIDDLE_PATCHES * a + i - 18), WHOLE
    r, j = divmod(i, 3)
    return (0, 1, 2, 2, 3, 4)[r], {(0, 0): LEFT, (1, 2): RIGHT}.get((a, j), WHOLE)


SEL_OUTER = TABLE * OUTER_W
SEL_MIDDLE_FIRST = -4
SEL_MIDDLE = 24 * MIDDLE_W
SEL_COLS = 24 * SEL_OUTER + 4 * SEL_MIDDLE
TABLE_SPLIT = 7
TABLE_PARTS = (TABLE_SPLIT * TABLE, (TABLE - TABLE_SPLIT) * TABLE)


def query_of(a, n, q, j):
    r, c = divmod(q, 4)
    if n < ROWS_OF_PATCHES:
        return 2 * n + r, 16 * a + 4 * j + c
    first = middle_tile(a, n)[0] - OUTER_PATCHES
    return 2 * (MIDDLE_PATCHES * a + first + j) + r, 12 + c


def selection_at(a, n, q, j):
    row, col = query_of(a, n, q, j)
    if n < ROWS_OF_PATCHES:
        first = 2 * outer_window(n) - 1
        return (12 * a + col - 16 * a) * SEL_OUTER + (first - row + WIN - 1) * OUTER_W
    first = middle_tile(a, n)[2]
    return 24 * SEL_OUTER + (col - 12) * SEL_MIDDLE + (first - row + WIN - 1 - SEL_MIDDLE_FIRST) * MIDDLE_W


C_ID, C_GROUP, C_HEAD, C_OUT, CONSTS = 0, 128, 256, 272, 276


BF16_ONE = 0x3F80


def constants():
    import numpy as np

    c = np.zeros((128, CONSTS), np.float32)
    window = np.zeros((128, BIAS_COLS // HEADS), np.float32)
    p = np.arange(128)
    c[:, C_ID:C_ID + 128] = np.eye(128)
    c[:, C_GROUP:C_GROUP + 128] = p[:, None] // NORM_GROUP == p[None] // NORM_GROUP
    c[:, C_HEAD:C_HEAD + HEADS] = (2 * (p % HEAD_PAIRS) + p // 64)[:, None] == np.arange(HEADS)[None]
    c[:, C_OUT:C_OUT + 4] = p[:, None] % 32 // HEAD_DIM == np.arange(4)[None]
    for a in range(2):
        for n, at, count in bias_kinds(a):
            if n < ROWS_OF_PATCHES:
                krow, kcol = 2 * outer_window(n) - 1 + p // OUTER_W, OUTER_COL[a] + p % OUTER_W
            else:
                krow, kcol = middle_tile(a, n)[2] + p // MIDDLE_W, MIDDLE_COL + p % MIDDLE_W
            for q in range(PATCH):
                for j in range(count):
                    row, col = query_of(a, n, q, j)
                    r0, c0 = (min(max(z - REACH, 0), SIDE - WIN) for z in (row, col))
                    seen = (krow >= r0) & (krow < r0 + WIN) & (kcol >= c0) & (kcol < c0 + WIN)
                    window[:, at // HEADS + q * count + j] = np.where(seen, 0.0, NEG)
    sel = np.zeros((2, 128, SEL_COLS), np.float32)
    for dh in range(TABLE):
        for dw in range(TABLE):
            part, entry = (0, dh * TABLE + dw) if dh < TABLE_SPLIT else (1, (dh - TABLE_SPLIT) * TABLE + dw)
            for a in range(2):
                for c12 in range(12):
                    k = dw - (WIN - 1) + 16 * a + c12 - OUTER_COL[a]
                    if 0 <= k < OUTER_W:
                        sel[part, entry, (12 * a + c12) * SEL_OUTER + dh * OUTER_W + k] = 1
            for c4 in range(4):
                k = dw - (WIN - 1) + 12 + c4 - MIDDLE_COL
                if 0 <= k < MIDDLE_W:
                    sel[part, entry, 24 * SEL_OUTER + c4 * SEL_MIDDLE + (dh - SEL_MIDDLE_FIRST) * MIDDLE_W + k] = 1
    return c, window, (sel * BF16_ONE).astype(np.uint16)


def build(nc, x, conv_w, w_qkv, b_qkv, rpb, w_proj, b_proj, const, window, select, out):
    F32, BF16 = mybir.dt.float32, mybir.dt.bfloat16
    ALU, ACT, AX = mybir.AluOpType, mybir.ActivationFunctionType, mybir.AxisListType
    SCALE = float(HEAD_DIM) ** -0.5

    x_mid = nc.dram_tensor("x_mid", (IMAGES, CH, POS), F32, kind="Internal").ap()
    q_parts = nc.dram_tensor("q_parts", (2, 2, len(PAIRS), HEAD_DIM, HEAD_PAIRS, 2 * CHUNK_Q), BF16, kind="Internal").ap()
    k_parts = nc.dram_tensor("k_parts", (2, 2, len(PAIRS), HEAD_DIM, HEAD_PAIRS, 2 * CHUNK_KEYS), BF16, kind="Internal").ap()
    sums = nc.dram_tensor("sums", (2, 8, 2 * CHUNK_Q), F32, kind="Internal").ap()

    ctx = ExitStack()
    with ctx:
        def sb(name, shape, dt=F32):
            return ctx.enter_context(nc.sbuf_tensor(name, shape, dt))

        cst = sb("cst", [128, CONSTS])
        identb = sb("identb", [128, 128], BF16)
        wqkv = sb("wqkv", [128, 3 * CH])
        wqk = sb("wqk", [128, 2, CH])
        bqkv = sb("bqkv", [128, 3])
        wproj = sb("wproj", [128, 2, CH])
        bproj = sb("bproj", [128, 1])
        scratch = sb("scratch", [128, 1])
        mv = sb("mv", [128, IMAGES, 2])
        small = sb("small", [128, 7, IMAGES])
        bias = sb("bias", [128, BIAS_COLS])
        biasp = sb("biasp", [128, 2, BIAS_PATCHES, PATCH_KEYS], BF16)
        S = sb("S", [128, 4, 512])
        VT = sb("VT", [128, 4, 4, 64])
        mcol = sb("mcol", [128, PATCHES], BF16)
        masked = sb("masked", [128, 2, 256])
        halves = sb("halves", [128, 2, 128])
        packed = sb("packed", [128, PATCHES])
        den = sb("den", [128, 2 * CHUNK_Q])
        xa = sb("xa", [128, POS])
        xn = sb("xn", [128, POS])
        yo = sb("yo", [128, POS])

        late = sb("late", [128, 2 * CHUNK_Q + SEL_COLS // 2])
        chosen = [sb("chosen0", [128, SEL_COLS], BF16)[:, :], late[:, 2 * CHUNK_Q:2 * CHUNK_Q + SEL_COLS // 2].bitcast(BF16)]
        sel = late[:, 0:4 * CHUNK_Q].rearrange("p (c g q t) -> p c g q t", c=2, g=2, q=PATCH)
        xr = late[:, 4 * CHUNK_Q:4 * CHUNK_Q + POS]
        area = [sb("area0", [128, IMAGES * POS]), sb("area1", [128, 13032])]

        def part(i, first, size, dt=F32):
            v = area[i][:, first:first + size]
            return v if dt == F32 else v.bitcast(dt)

        X = area[0][:, :].rearrange("p (i n) -> p i n", n=POS)
        wconv = part(1, 0, 9 * CH).rearrange("p (t c) -> p t c", t=9)
        padded = [part(1, 1152 + i * PAD * PAD, PAD * PAD) for i in range(2)]
        xin = [part(1, 2952 + i * 896, 896)[0:PIECE].rearrange("p (k c) -> p k c", k=PIECES) for i in range(2)] + [
            part(1, 11048 + i * 896, 896)[0:PIECE].rearrange("p (k c) -> p k c", k=PIECES) for i in range(2)]
        seen = part(1, 7168, BIAS_COLS // HEADS)
        stats = yo[:, 0:12 * IMAGES].rearrange("p (i k) -> p i k", k=12)
        table = [sel[0:TABLE_PARTS[i], 0, i, 0, 0:HEADS] for i in range(2)]
        tparts = [masked[0:TABLE_PARTS[i], i, 0:24].bitcast(BF16) for i in range(2)]
        trest = [halves[0:TABLE_PARTS[i], i, 0:HEADS] for i in range(2)]
        biasb = [S[:, 0, 64 * i:64 * i + 64].bitcast(BF16) for i in range(8)]

        KP, QP = HEAD_PAIRS * CHUNK_KEYS // 2, HEAD_PAIRS * CHUNK_Q
        key_rows = [part(0, i * KP, KP, BF16).rearrange("p (g k) -> p g k", g=HEAD_PAIRS) for i in range(2)]
        query_rows = [part(0, 2 * KP + i * QP, QP, BF16).rearrange("p (g h q t) -> p g h q t", g=HEAD_PAIRS, h=2, q=PATCH)
                      for i in range(2)]
        ot = part(0, 2 * (KP + QP), PIECES * CH)[0:PIECE].rearrange("p (k c) -> p k c", k=PIECES)
        Qbd = part(1, 0, 3136, BF16).rearrange("p (h q t) -> p h q t", h=HEADS, q=PATCH)
        kf = part(1, 3136, 2 * CHUNK_KEYS).rearrange("p (a k) -> p a k", a=2)
        k1 = [part(1, 4480 + i * CHUNK_KEYS, CHUNK_KEYS, BF16) for i in range(2)]
        k23 = [part(1, 5824 + i * CHUNK_KEYS, CHUNK_KEYS, BF16) for i in range(2)]
        normed = part(1, 7520, 2 * CHUNK_Q)
        V = [part(1, 8512 + i * VALUES, VALUES) for i in range(2)]
        qf = part(1, 11072, POS)
        qparts = [part(1, 11856 + i * CHUNK_Q, CHUNK_Q, BF16) for i in range(3)]

        KINDS = [(a, n, at, count) for a in range(2) for n, at, count in bias_kinds(a)]

        def turned_bias(k):
            return PS[:, k % 8, 0:64].bitcast(BF16)

        PS = ctx.enter_context(nc.psum_tensor("PS", [128, 8, 512], F32))
        SCORE, SUM, VALUE, PEAK, MISC = 0, 2, 4, 5, 6

        ROWS_IN = 16 * 4

        CREDIT = {"xin_kept": X_RING, "conv_added": 4, "weighted": 4, "selected": 2, "half": 2,
                  "value_out": 1, "summed": 1, "normed": 1, "out_done": 1}
        EACH = {"misc_in": 20, "misc_out": 20, "rows_in": 4 * ROWS_IN, "middle_in": 64, "scores": 64, "biased": 64, "probs": 64,
                "weighted": 64, "selected": 64, "half": 64, "summed": 64, "qbd": 4, "qbd_too": 4, "peak_in": 4 * CHUNK_BANKS,
                "peak_out": 4 * CHUNK_BANKS, "value_in": 4 * WINDOWS, "value_out": 4 * WINDOWS,
                "lead": 6, "rest": 12, "second": 6, "third": 12, "k_stored": 192, "q_stored": 192,
                "sums_out": 128, "packed_in": 64, "recip": 4, "recip_out": 64, "den_in": 128, "normed": 4,
                "xa_in": 32, "xr_in": 32, "residual": 2, "out_done": 32, "xn_ready": 2}
        s = {name: ctx.enter_context(nc.semaphore("s_" + name)) for name in (
            *EACH, "init", "spaces", "weights", "scratch", "warm", "cleared", "x_mid_out", "pool_loaded", "const_in", "loaded",
            "xin_in0", "xin_in1", "xin_in2", "xin_in3", "xin_turned", "xin_kept", "table_in", "table_split",
            "table_picked", "table_kept", "rounded", "turned", "placed", "dve_chain", "mean_in", "mean_sum", "var_in",
            "var_sum", "sqrt_in", "sqrt_out", "padded_ready", "conv", "conv_added", "first_stats")}

        def wait(eng, name, k, j=None, each=None):
            k += CREDIT.get(name, 0)
            assert k >= 0 if j is None else k > 0, (name, k)
            eng.wait_ge(s[name], k if j is None else j * (each or EACH[name]) + k)

        ident, group = cst[:, C_ID:C_ID + 128], cst[:, C_GROUP:C_GROUP + 128]
        MEAN, RSTD = 0, 1
        INITS, SPACES, WEIGHTS = 10, 5, 3
        SMALL_LOADS, POOL_LOADS = 16 * 5, 16 * (4 + 9 + 2 + 1)
        MISC_IMAGE, MISC_FIRST = 10, 6
        block = ctx.enter_context(nc.Block())

        Q, KEY, VAL = range(3)
        PROJECTED = {0: (KEY, 0), 1: (KEY, 1), 3: (Q, 0), 5: (Q, 1), 26: (VAL, 0), 28: (VAL, 1)}
        MISC_PROJECT, MISC_TURN = 13, 24
        SPREAD = ({12: (0, 1), 13: (2,), 14: (3,), 15: (4,), 0: (8, 9, 10), 1: (11, 12, 13), 2: (14, 15)},
                  {12: (0,), 13: (1,), 14: (2,), 15: (3,), 0: (9, 10), 1: (12, 13), 2: (14, 15)})
        SPREAD_TOO = ({12: (5,), 13: (6, 7)}, {12: (4,), 13: (5,), 14: (6, 7), 0: (8,), 1: (11,)})

        def spread_for(split, a, late):
            return [h for n, heads in split[1 - a if late else a].items() for h in heads if (n < 12) == late]

        FIRST_BANK, RECIPROCAL, NORMALIZE, NEXT_IMAGE, RESIDUAL = 3, 6, 12, 30, 20
        K_PIECE, Q_PIECE = CHUNK_KEYS // 2, CHUNK_Q
        LEAD = {3: ("k", 0), 5: ("k", 1), 7: ("q", 0)}
        SECOND = {8: ("k", 0), 10: ("k", 1), 14: ("q", 0)}
        REST = {4: ("k", 0), 5: ("k", 1), 6: ("k", 2), 7: ("k", 3), 8: ("q", 0), 9: ("q", 1)}
        THIRD = {10: ("k", 0), 11: ("k", 1), 12: ("k", 2), 13: ("k", 3), 17: ("q", 0), 18: ("q", 1)}

        def misc_project(c):
            return MISC_FIRST + MISC_IMAGE * (c // 2) + (9 if c % 2 else 4 if c < 2 * IMAGES else 0)

        def misc_qkv(i, which, half):
            at = 2 * (KEY, Q, VAL).index(which) + half
            return MISC_IMAGE * (i - 1) + MISC_FIRST + at + (3 if which == VAL else 0) if i else at

        def misc_turn(i, part):
            return MISC_FIRST + MISC_IMAGE * i + (5 if i < IMAGES else 1) + part

        def new_window(n):
            w = tile_of(0, n)[4]
            return w if n == 0 or tile_of(0, n - 1)[4] != w else None

        def window_for_next(c, n):
            c, n = (c, n + 1) if n + 1 < TILES else (c + 1, 0)
            w = new_window(n)
            return None if w is None else (c, n, WINDOWS * c + w)

        def tiles_until(w):
            c, k = divmod(w, WINDOWS)
            return TILES * c + max(n for n in range(TILES) if tile_of(0, n)[4] == k) + 1

        @block.sync
        def _(sp):
            for b in range(X_RING):
                sp.dma_start(xin[b], x[b].rearrange("(k p) c -> p k c", p=PIECE)).then_inc(s[f"xin_in{b}"], 16)
            sp.dma_start(cst[:, :], const).then_inc(s["const_in"], 16)
            sp.dma_start(wqkv[:, :], w_qkv).then_inc(s["loaded"], 16)
            for k in range(3):
                order = "(g l d o) -> l d g o" if k < 2 else "(l d g o) -> l d g o"
                sp.dma_start(bqkv[:, k:k + 1], b_qkv[CH * k:CH * (k + 1)].rearrange(order, l=2, d=HEAD_DIM, o=1),
                             allow_slow_non_contiguous=True).then_inc(s["loaded"], 16)
            sp.dma_start(bproj[:, :], b_proj.rearrange("(p o) -> p o", o=1)).then_inc(s["loaded"], 16)
            with nc.sync.Fori(0, IMAGES // X_RING - 1) as j:
                for b in range(X_RING):
                    wait(sp, "xin_turned", b + 1, j, X_RING)
                    sp.dma_start(xin[b], x[X_RING * j + X_RING + b].rearrange("(k p) c -> p k c", p=PIECE)
                                 ).then_inc(s[f"xin_in{b}"], 16)

            with nc.sync.Fori(0, IMAGES // 2) as j:
                for b in range(2):
                    wait(sp, "conv_added", 2 * b + 2, j, 4)
                    sp.dma_start(x_mid[2 * j + b], X[:, 2 * j + b, :]).then_inc(s["x_mid_out"], 16)

            def load_next(img):
                sp.dma_start(xa[:, :], x_mid[img]).then_inc(s["xa_in"], 16)

            def load_residual(img):
                sp.dma_start(xr[:, :], x_mid[img]).then_inc(s["xr_in"], 16)

            def store_parts(j, i, third):
                def store(parts, to, pair, slots, done):
                    for slot in slots:
                        sp.dma_start(to.rearrange("l s d g n -> s l (d g) n")[slot], parts[PAIRS[slot][pair]]
                                     ).then_inc(s[done], 16)

                keys = ((k1[i % 2], k23[0], k23[1]), k_parts[i % 2], 1)
                queries = (qparts, q_parts[i % 2], 0)
                slots = [[slot for slot, pair in enumerate(PAIRS) if (pair[which] == 2) == third] for which in range(2)]
                if third:
                    wait(sp, "third", 6 * i + 6, j)
                else:
                    wait(sp, "second", 3 * i + 2, j)
                store(*keys, slots[1], "k_stored")
                if not third:
                    wait(sp, "second", 3 * i + 3, j)
                store(*queries, slots[0], "q_stored")

            def fill_queries(j, c):
                if c % 2 == 0:
                    wait(sp, "q_stored", 96 * (c // 2 + 1), j)
                for l in range(2):
                    sp.dma_start(query_rows[c % 2][HEAD_ROWS * l:HEAD_ROWS * (l + 1), :, l, :, :].rearrange("r g q t -> r g (q t)"),
                                 q_parts[c // 2 % 2, l].rearrange("s d g (a n) -> a (s d) g n", a=2)[c % 2]
                                 ).then_inc(s["rows_in"], 16)

            def fill_keys(j, c):
                if c % 2 == 0:
                    wait(sp, "k_stored", 96 * (c // 2 + 1), j)
                sp.dma_start(key_rows[c % 2][0:PEAK_ROW],
                             k_parts[c // 2 % 2].rearrange("l s d g (a n) -> a (l s d) g n", a=2)[c % 2]
                             ).then_inc(s["rows_in"], 16)

            def move_maxima(j, c, middle):
                banks, patches = ((CHUNK_BANKS, slice(OUTER_PATCHES, PATCHES)) if middle
                                  else (CHUNK_BANKS - 2, slice(0, OUTER_PATCHES)))
                wait(sp, "peak_out", c * CHUNK_BANKS + banks, j)
                row = query_rows[c % 2][PEAK_ROW:PEAK_ROW + 1].rearrange("o g h q t -> o (g h q) t")
                sp.dma_start(row[:, :, patches], mcol[:, patches]).then_inc(s["middle_in" if middle else "rows_in"], 16)

            def collect_denominators(j, c):
                to = sums[(c + 1) % 2]
                wait(sp, "summed", TILES * c, j)
                for g in range(2):
                    sp.dma_start(to[4 * g:4 * g + 4, :],
                                 sel[64 * g + 32:64 * g + 64:HEAD_DIM, (c + 1) % 2, :, :, :].rearrange("p g q t -> p (g q t)")
                                 ).then_inc(s["sums_out"], 16)
                wait(sp, "sums_out", 32 * (c + 1), j)
                sp.dma_start(packed[:, :], to.rearrange("h n -> (h n)").rearrange("(p n) -> p n", p=128)
                             ).then_inc(s["packed_in"], 16)

            def spread_reciprocals(j, c):
                to = sums[(c + 1) % 2]
                wait(sp, "recip", c + 1, j)
                sp.dma_start(to.rearrange("h n -> (h n)").rearrange("(p n) -> p n", p=128), packed[:, :]
                             ).then_inc(s["recip_out"], 16)
                wait(sp, "recip_out", 16 * (c + 1), j)
                for g in range(2):
                    src = to[4 * g:4 * g + 4, :].unsqueeze(1).broadcast_to([4, HEAD_DIM, 2 * CHUNK_Q])
                    sp.dma_start(den[64 * g:64 * g + 32, :], src).then_inc(s["den_in"], 16)

            def store(j, i, img):
                wait(sp, "misc_out", misc_turn(i, 1) + 1, j)
                sp.dma_start(out[img].rearrange("(k p) c -> p k c", p=PIECE), ot[:, :, :]).then_inc(s["out_done"], 16)

            sp.wait_ge(s["x_mid_out"], 16 * IMAGES)
            load_next(0)
            sp.wait_ge(s["spaces"], SPACES)
            store_parts(None, 0, False)
            store_parts(None, 0, True)
            sp.wait_ge(s["xn_ready"], 1)
            load_next(1)
            fill_queries(None, 0)
            fill_keys(None, 0)
            sp.wait_ge(s["table_picked"], len(KINDS))
            load_residual(IMAGES - 1)
            move_maxima(None, 0, False)
            move_maxima(None, 0, True)
            sp.wait_ge(s["scores"], 1)
            with nc.sync.Fori(0, IMAGES // 2) as j:
                for c in range(4):
                    i = c // 2
                    collect_denominators(j, c)
                    if c % 2:
                        store_parts(j, i + 1, True)
                    else:
                        fill_queries(j, c + 1)
                    spread_reciprocals(j, c)
                    fill_keys(j, c + 1)
                    if c % 2:
                        fill_queries(j, c + 1)
                    move_maxima(j, c + 1, False)
                    move_maxima(j, c + 1, True)
                    if c % 2 == 0:
                        load_next((2 * j + i + 2) % IMAGES)
                        store_parts(j, i + 1, False)
                    else:
                        store(j, i, (2 * j + i + IMAGES - 1) % IMAGES)
                        load_residual(2 * j + i)
            collect_denominators(None, 2 * IMAGES)
            spread_reciprocals(None, 2 * IMAGES)
            store(None, IMAGES, IMAGES - 1)
            wait(sp, "out_done", 16 * (IMAGES + 1))

        @block.gpsimd
        def _(pool):
            nc.gpsimd.memset(wproj[:, :, :], 0.0).then_inc(s["cleared"], 1)
            for ap, value in ((padded[0], 0.0), (padded[1], 0.0), (den[:, :], 1.0)):
                nc.gpsimd.memset(ap, value).then_inc(s["cleared"], 1)
            pool.wait_ge(s["cleared"], 1)
            for g in range(4):
                pool.dma_start(wproj[64 * (g % 2):64 * (g % 2) + 32, g // 2, :], w_proj[32 * g:32 * g + 32, :]
                               ).then_inc(s["pool_loaded"], 16)
            for tap in range(9):
                pool.dma_start(wconv[:, tap, :], conv_w[tap // 3, tap % 3].unsqueeze(0).broadcast_to([CH // NORM_GROUP, NORM_GROUP, CH])
                               ).then_inc(s["pool_loaded"], 16)
            for i in range(2):
                pool.dma_start(chosen[i], select[i].bitcast(BF16)).then_inc(s["pool_loaded"], 16)
            pool.dma_start(seen, window).then_inc(s["pool_loaded"], 16)
            for i in range(2):
                first = TABLE_SPLIT * i
                rows = rpb[:, first:first + TABLE_PARTS[i] // TABLE, :]
                pool.dma_start(table[i], rows.rearrange("h a b -> (a b) h"), allow_slow_non_contiguous=True).then_inc(s["table_in"], 16)
            pool.wait_ge(s["first_stats"], 4 * IMAGES)
            pool.wait_ge(s["padded_ready"], IMAGES + 2)
            pool.wait_ge(s["x_mid_out"], 16 * IMAGES)
            for ap in (kf, V[0], V[1]):
                nc.gpsimd.memset(ap, 0.0).then_inc(s["spaces"], 1)
            for a in range(2):
                nc.gpsimd.memset(part(0, 2 * KP + a * QP, QP), 0.0).then_inc(s["spaces"], 1)

            def add_heads(j, c, n):
                t0, count = tile_of(c % 2, n)[:2]
                T = TILES * c + n
                q = PATCH * count
                wait(pool, "selected", T + 1, j)
                if n == 0:
                    wait(pool, "normed", c, j)
                m = masked[:, n % 2, 0:8 * q].rearrange("p (g h q) -> p g h q", g=2, h=4)
                h = halves[:, n % 2, 0:4 * q].rearrange("p (g h q) -> p g h q", g=2, h=2)
                nc.gpsimd.tensor_tensor(h, m[:, :, 0:2, :], m[:, :, 2:4, :], ALU.add).then_inc(s["half"], 1)
                wait(pool, "half", T + 1, j)
                h = halves[:, n % 2, 0:4 * q].rearrange("p (g h a t) -> p g h a t", g=2, h=2, a=PATCH)
                nc.gpsimd.tensor_tensor(sel[:, c % 2, :, :, t0:t0 + count], h[:, :, 0], h[:, :, 1], ALU.add
                                        ).then_inc(s["summed"], 1)

            def add_residual(j, i, img):
                wait(pool, "misc_out", misc_project(2 * i) + 1, j)
                wait(pool, "xr_in", 16 * (i + 1), j)
                nc.gpsimd.tensor_tensor(yo[:, :], yo[:, :], xr[:, :], ALU.add).then_inc(s["residual"], 1)

            def subtract_lead(j, i, kind, piece):
                a, h = divmod(piece, 2)
                if kind == "k":
                    wait(pool, "lead", 3 * i + a + 1, j)
                    v, at = kf[:, a, :], slice(K_PIECE * h, K_PIECE * (h + 1))
                    lead = k1[i % 2][:, CHUNK_KEYS * a + at.start:CHUNK_KEYS * a + at.stop]
                else:
                    wait(pool, "lead", 3 * i + 3, j)
                    v, at = qf, slice(Q_PIECE * piece, Q_PIECE * (piece + 1))
                    lead = qparts[0][:, at]
                nc.gpsimd.tensor_tensor(v[:, at], v[:, at], lead, ALU.subtract).then_inc(s["rest"], 1)

            def subtract_second(j, i, kind, piece):
                a, h = divmod(piece, 2)
                if kind == "k":
                    wait(pool, "second", 3 * i + a + 1, j)
                    at = slice(CHUNK_KEYS * a + K_PIECE * h, CHUNK_KEYS * a + K_PIECE * (h + 1))
                    v, second, third = kf[:, a, K_PIECE * h:K_PIECE * (h + 1)], k23[0][:, at], k23[1][:, at]
                else:
                    wait(pool, "second", 3 * i + 3, j)
                    at = slice(Q_PIECE * piece, Q_PIECE * (piece + 1))
                    v, second, third = qf[:, at], qparts[1][:, at], qparts[2][:, at]
                nc.gpsimd.tensor_tensor(third, v, second, ALU.subtract).then_inc(s["third"], 1)

            for step in REST.values():
                subtract_lead(None, 0, *step)
            for step in THIRD.values():
                subtract_second(None, 0, *step)
            pool.wait_ge(s["table_picked"], len(KINDS))
            nc.gpsimd.memset(sel[:, 1, :, :, :], 1.0).then_inc(s["init"], 1)
            pool.wait_ge(s["mean_in"], 2)
            nc.gpsimd.memset(yo[:, :], 0.0).then_inc(s["init"], 1)
            pool.wait_ge(s["init"], INITS)
            with nc.gpsimd.Fori(0, IMAGES // 2) as j:
                for c in range(4):
                    for n in range(TILES):
                        add_heads(j, c, n)
                        step = n + TILES * (c % 2)
                        if step in REST:
                            subtract_lead(j, c // 2 + 1, *REST[step])
                        if step in THIRD:
                            subtract_second(j, c // 2 + 1, *THIRD[step])
                        if step == RESIDUAL:
                            add_residual(j, c // 2, (2 * j + c // 2 + IMAGES - 1) % IMAGES)
            add_residual(None, IMAGES, IMAGES - 1)

        @block.scalar
        def _(act):
            act.wait_ge(s["scratch"], 1)
            nc.scalar.activation(scratch[:, 0:1], scratch[:, 0:1], ACT.Copy).then_inc(s["warm"], 1)
            with nc.scalar.Fori(0, IMAGES // X_RING) as j:
                for b in range(X_RING):
                    wait(act, "xin_turned", b + 1, j, X_RING)
                    nc.scalar.activation(X[:, X_RING * j + b, 0:448], PS[:, 2 * b, 0:448], ACT.Copy)
                    nc.scalar.activation(X[:, X_RING * j + b, 448:784], PS[:, 2 * b + 1, 0:336], ACT.Copy
                                         ).then_inc(s["xin_kept"], 1)
            for k in range(2):
                act.wait_ge(s["sqrt_in"], k + 1)
                nc.scalar.activation(small[:, 4, :], small[:, 3, :], ACT.Sqrt).then_inc(s["sqrt_out"], 1)
            act.wait_ge(s["loaded"], SMALL_LOADS)
            nc.scalar.mul(bqkv[:, 0:1], bqkv[:, 0:1], SCALE).then_inc(s["weights"], 1)
            for which in range(2):
                nc.scalar.activation(wqk[:, which, :].rearrange("p (l d g) -> p l d g", l=2, d=HEAD_DIM),
                                     wqkv[:, CH * which:CH * (which + 1)].rearrange("p (g l d) -> p l d g", l=2, d=HEAD_DIM),
                                     ACT.Copy).then_inc(s["weights"], 1)

            def misc(j, k):
                wait(act, "misc_in", k + 1, j)
                return PS[:, MISC + k % 2, 0:HALF]

            def keep(dst, src, func, **kw):
                for d, p in zip(dst, src):
                    last = nc.scalar.activation(d, p, func, **kw)
                last.then_inc(s["misc_out"], 1)

            def keep_qkv(j, i, which, half):
                p = misc(j, misc_qkv(i, which, half)).rearrange("p (r c) -> p r c", c=SIDE)
                if which == Q:
                    dst, src = [], []
                    pr = p.rearrange("p (t r) c -> p t r c", r=2)
                    q = qf.rearrange("p (a q t) -> p a q t", a=2, q=PATCH)
                    for r in range(2):
                        for a in range(2):
                            o = q[:, a, 4 * r:4 * r + 4, 21 * half:21 * half + 21]
                            dst.append(o.rearrange("p c (t j) -> p t j c", j=3))
                            src.append(pr[:, :, r, 16 * a:16 * a + 12].rearrange("p t (j c) -> p t j c", j=3))
                    dst.append(q[:, half, :, OUTER_PATCHES:PATCHES].rearrange("p (r c) t -> p r t c", r=2))
                    src.append(pr[:, :, :, 12:16].rearrange("p t r c -> p r t c"))
                    if i and half == 0:
                        wait(act, "third", 6 * i, j)
                    keep(dst, src, ACT.Identity, scale=SCALE, bias=bqkv[:, 0:1])
                    return
                inner = slice(1 + HALF_ROWS * half, 1 + HALF_ROWS * (half + 1))
                all_rows = slice(0, HALF_ROWS)
                dst, src = [], []

                def piece(buf, w, col, to, rows):
                    dst.append(buf.rearrange("p (r c) -> p r c", c=w)[:, to, :])
                    src.append(p[:, rows, col:col + w])

                for a in range(2):
                    buf = kf[:, a, 0:STRIP] if which == KEY else V[i % 2][:, a * STRIP:(a + 1) * STRIP]
                    piece(buf, OUTER_W, OUTER_COL[a], inner, all_rows)
                if which == VAL:
                    piece(V[i % 2][:, MIDDLE_AT:MIDDLE_AT + PAD * MIDDLE_W], MIDDLE_W, MIDDLE_COL, inner, all_rows)
                else:
                    for a in range(2):
                        first = max(inner.start, MIDDLE_FIRST[a])
                        last = min(inner.stop, MIDDLE_FIRST[a] + MIDDLE_ROWS)
                        piece(kf[:, a, STRIP:STRIP + MIDDLE_ROWS * MIDDLE_W], MIDDLE_W, MIDDLE_COL,
                              slice(first - MIDDLE_FIRST[a], last - MIDDLE_FIRST[a]),
                              slice(first - inner.start, last - inner.start))
                    if i and half == 0:
                        wait(act, "third", 6 * i - 2, j)
                keep(dst, src, ACT.Identity, bias=bqkv[:, which:which + 1])

            def keep_lead(j, i, kind, a):
                if kind == "k":
                    wait(act, "misc_out", misc_qkv(i, KEY, 1) + 1, j)
                    dst, src = k1[i % 2][:, CHUNK_KEYS * a:CHUNK_KEYS * (a + 1)], kf[:, a, :]
                else:
                    wait(act, "misc_out", misc_qkv(i, Q, 1) + 1, j)
                    if i:
                        wait(act, "qbd", 2 * i, j)
                    dst, src = qparts[0], qf
                nc.scalar.activation(dst, src, ACT.Copy).then_inc(s["lead"], 1)

            def keep_second(j, i, kind, a):
                if kind == "k":
                    wait(act, "rest", 6 * i + 2 * (a + 1), j)
                    dst, src = k23[0][:, CHUNK_KEYS * a:CHUNK_KEYS * (a + 1)], kf[:, a, :]
                else:
                    wait(act, "rest", 6 * i + 6, j)
                    dst, src = qparts[1], qf
                nc.scalar.activation(dst, src, ACT.Copy).then_inc(s["second"], 1)

            def spread_too(j, c, heads):
                order = spread_for(SPREAD_TOO, c % 2, False) + spread_for(SPREAD_TOO, c % 2, True)
                if heads[0] == order[0]:
                    wait(act, "lead", 3 * (c // 2) + 3, j)
                    if c:
                        wait(act, "peak_in", CHUNK_BANKS * c, j)
                for h in heads:
                    last = nc.scalar.activation(Qbd[:, h, :, :], qparts[0].rearrange("p (a q t) -> p a q t", a=2, q=PATCH)[:, c % 2],
                                                ACT.Copy, scale=cst[:, C_HEAD + h:C_HEAD + h + 1])
                if heads[-1] == order[-1]:
                    last.then_inc(s["qbd_too"], 1)

            def keep_value(j, w):
                wait(act, "value_in", w + 1, j)
                if j is not None:
                    wait(act, "weighted", tiles_until(w - 4), j)
                nc.scalar.activation(VT[:, w % 4, :, 0:32],
                                     PS[:, VALUE, 0:128].rearrange("p (g c) -> p g c", g=4),
                                     ACT.Copy).then_inc(s["value_out"], 1)

            def exponentials(j, c, n):
                cols = HEADS * PATCH * tile_of(c % 2, n)[1]
                wait(act, "biased", TILES * c + n + 1, j)
                nc.scalar.activation(S[:, n % 4, 0:cols], S[:, n % 4, 0:cols], ACT.Exp).then_inc(s["probs"], 1)

            def keep_projection(j, c):
                a = (c + 1) % 2
                p = misc(j, misc_project(c)).rearrange("p (q t) -> p q t", q=PATCH)
                img = yo[:, :].rearrange("p (t r c) -> p t r c", r=2, c=SIDE)
                dst, src = [], []
                for r in range(2):
                    for half in range(2):
                        dst.append(img[:, 7 * half:7 * half + 7, r, 16 * a:16 * a + 12].rearrange("p t (j c) -> p t j c", j=3))
                        src.append(p[:, 4 * r:4 * r + 4, 21 * half:21 * half + 21].rearrange("p c (t j) -> p t j c", j=3))
                dst.append(img[:, 7 * a:7 * a + 7, :, 12:16].rearrange("p t r c -> p r t c"))
                src.append(p[:, :, OUTER_PATCHES:PATCHES].rearrange("p (r c) t -> p r t c", r=2))
                keep(dst, src, ACT.Identity, bias=bproj[:, 0:1])

            def keep_turned(j, i, part):
                k = misc_turn(i, part)
                misc(j, k)
                if part == 0:
                    wait(act, "out_done", 16 * i, j)
                count = 4 - part
                keep([ot[:, 4 * part:4 * part + count, :]],
                     [PS[0:PIECE, MISC + k % 2, 0:CH * count].rearrange("p (k c) -> p k c", c=CH)], ACT.Copy)

            act.wait_ge(s["spaces"], SPACES)
            act.wait_ge(s["warm"], 1)
            nc.scalar.activation(scratch[:, 0:1], scratch[:, 0:1], ACT.Exp)
            for which in (KEY, Q, VAL):
                for half in range(2):
                    keep_qkv(None, 0, which, half)
            for step in LEAD.values():
                keep_lead(None, 0, *step)
            spread_too(None, 0, spread_for(SPREAD_TOO, 0, False) + spread_for(SPREAD_TOO, 0, True))
            for step in SECOND.values():
                keep_second(None, 0, *step)
            for a in range(2):
                row = key_rows[a][PEAK_ROW:PEAK_ROW + 1].rearrange("p g k -> p (g k)")
                one = cst[PEAK_ROW:PEAK_ROW + 1, C_ID + PEAK_ROW:C_ID + PEAK_ROW + 1]
                nc.scalar.activation(row, one.broadcast_to([1, HEAD_PAIRS * CHUNK_KEYS]), ACT.Copy, scale=-1.0
                                     ).then_inc(s["init"], 1)
            act.wait_ge(s["init"], INITS)
            keep_value(None, 0)
            spread_too(None, 1, spread_for(SPREAD_TOO, 1, False))
            with nc.scalar.Fori(0, IMAGES // 2) as j:
                for c in range(4):
                    for n in range(TILES):
                        exponentials(j, c, n)
                        window = window_for_next(c, n)
                        if window:
                            keep_value(j, window[2])
                        step = n + TILES * (c % 2)
                        if n == MISC_PROJECT + 2:
                            keep_projection(j, c)
                        if step - 1 in PROJECTED:
                            keep_qkv(j, c // 2 + 1, *PROJECTED[step - 1])
                        if MISC_TURN < step <= MISC_TURN + 2:
                            keep_turned(j, c // 2, step - 1 - MISC_TURN)
                        if step in LEAD:
                            keep_lead(j, c // 2 + 1, *LEAD[step])
                        if step in SECOND:
                            keep_second(j, c // 2 + 1, *SECOND[step])
                        if n in SPREAD_TOO[c % 2]:
                            spread_too(j, c + 2 if n >= 12 else c + 1, SPREAD_TOO[c % 2][n])
            keep_projection(None, 2 * IMAGES)
            for part in range(2):
                keep_turned(None, IMAGES, part)

        @block.vector
        def _(dve):
            dve_steps = [0]

            def link(ins):
                dve_steps[0] += 1
                ins.then_inc(s["dve_chain"], 1)
                dve.wait_ge(s["dve_chain"], dve_steps[0])

            nc.vector.memset(scratch[:, :], 0.0).then_inc(s["scratch"], 1)
            for w in range(4):
                nc.vector.memset(VT[:, w, :, :], 1.0).then_inc(s["init"], 1)
            for i, (name, credit) in enumerate(CREDIT.items()):
                nc.vector.memset(small[:, 6, i:i + 1], 0.0).then_inc(s[name], credit)
            dve.wait_ge(s["const_in"], 16)
            nc.vector.tensor_copy(identb[:, :], ident).then_inc(s["init"], 1)

            with nc.vector.Fori(0, IMAGES // 2) as j:
                for b in range(2):
                    wait(dve, "xin_kept", b + 1, j, 2)
                    for half in range(2):
                        nc.vector.bn_stats(stats[:, 2 * j + b, 6 * half:6 * half + 6],
                                           X[:, 2 * j + b, HALF * half:HALF * half + HALF]).then_inc(s["first_stats"], 1)

            def group_norm_terms(k, stats_done):
                dve.wait_ge(s["first_stats"], stats_done)
                for i in range(IMAGES):
                    last = nc.vector.bn_aggr(mv[:, i, :], stats[:, i, :].rearrange("p (h k) -> p h k", k=6))
                last.then_inc(s["mean_in"], 1)
                dve.wait_ge(s["mean_sum"], k + 1)
                link(nc.vector.tensor_scalar(small[:, MEAN, :], PS[:, PEAK, 0:IMAGES], 1.0 / NORM_GROUP, None, ALU.mult))
                dve.wait_ge(s["mean_in"], k + 1)
                link(nc.vector.tensor_tensor(small[:, 2, :], mv[:, :, 0], small[:, MEAN, :], ALU.subtract))
                link(nc.vector.tensor_tensor(small[:, 3, :], small[:, 2, :], small[:, 2, :], ALU.mult))
                nc.vector.tensor_tensor(small[:, 2, :], small[:, 3, :], mv[:, :, 1], ALU.add).then_inc(s["var_in"], 1)
                dve.wait_ge(s["var_sum"], k + 1)
                nc.vector.tensor_scalar(small[:, 3, :], PS[:, PEAK, 0:IMAGES], 1.0 / NORM_GROUP, 1e-5, ALU.mult, ALU.add
                                        ).then_inc(s["sqrt_in"], 1)
                dve.wait_ge(s["sqrt_in"], k + 1)
                dve.wait_ge(s["sqrt_out"], k + 1)
                link(nc.vector.reciprocal(small[:, 5, :], small[:, 4, :]))
                link(nc.vector.tensor_tensor(small[:, 6, :], small[:, 5, :], small[:, 5, :], ALU.mult))
                link(nc.vector.tensor_tensor(small[:, 6, :], small[:, 6, :], small[:, 3, :], ALU.mult))
                link(nc.vector.tensor_scalar(small[:, 6, :], small[:, 6, :], -0.5, 1.5, ALU.mult, ALU.add))
                link(nc.vector.tensor_tensor(small[:, RSTD, :], small[:, 5, :], small[:, 6, :], ALU.mult))

            def normalize(dst, src, img, done):
                nc.vector.tensor_scalar(dst, src.rearrange("p (r c) -> p r c", c=SIDE),
                                        small[:, MEAN, :].unsqueeze(2)[:, img, :], small[:, RSTD, :].unsqueeze(2)[:, img, :],
                                        ALU.subtract, ALU.mult).then_inc(s[done], 1)

            group_norm_terms(0, 2 * IMAGES)

            dve.wait_ge(s["cleared"], 4)
            inner = [padded[b].rearrange("p (r c) -> p r c", c=PAD)[:, 1:1 + SIDE, 1:1 + SIDE] for b in range(2)]
            dve.wait_ge(s["pool_loaded"], POOL_LOADS)
            link(nc.vector.tensor_tensor(wconv, wconv, group.unsqueeze(1).broadcast_to([128, 9, CH]), ALU.mult))
            normalize(inner[0], X[:, 0, :], 0, "padded_ready")
            normalize(inner[1], X[:, 1, :], 1, "padded_ready")
            with nc.vector.Fori(0, IMAGES // 2) as j:
                for b in range(2):
                    for half in range(2):
                        wait(dve, "conv", 2 * b + half + 1, j, 4)
                        xh = X[:, 2 * j + b, HALF * half:HALF * half + HALF]
                        nc.vector.tensor_tensor(xh, xh, PS[:, 2 * b + half, 0:HALF], ALU.add).then_inc(s["conv_added"], 1)
                    img = (2 * j + b + 2) % IMAGES
                    normalize(inner[b], X[:, img, :], img, "padded_ready")
                    for half in range(2):
                        wait(dve, "conv_added", 2 * b + half + 1, j, 4)
                        xh = X[:, 2 * j + b, HALF * half:HALF * half + HALF]
                        nc.vector.bn_stats(stats[:, 2 * j + b, 6 * half:6 * half + 6], xh).then_inc(s["first_stats"], 1)
            dve.wait_ge(s["padded_ready"], IMAGES + 2)
            group_norm_terms(1, 4 * IMAGES)

            def next_image(j, i, img):
                wait(dve, "xa_in", 16 * (i + 1), j)
                if i:
                    wait(dve, "misc_in", misc_qkv(i - 1, VAL, 1) + 1, j)
                normalize(xn[:, :].rearrange("p (r c) -> p r c", c=SIDE), xa[:, :], img, "xn_ready")

            next_image(None, 0, 0)

            dve.wait_ge(s["table_in"], 32)
            for i in range(2):
                parts = [tparts[i][:, HEADS * k:HEADS * k + HEADS] for k in range(3)]
                link(nc.vector.tensor_copy(parts[0], table[i]))
                link(nc.vector.tensor_tensor(trest[i], table[i], parts[0], ALU.subtract))
                link(nc.vector.tensor_copy(parts[1], trest[i]))
                nc.vector.tensor_tensor(parts[2], trest[i], parts[1], ALU.subtract).then_inc(s["table_split"], 1)
            for k, (a, n, at, count) in enumerate(KINDS):
                dve.wait_ge(s["table_picked"], k + 1)
                banks = PS[:, 4 * (k % 2):4 * (k % 2) + 4, :]
                to = bias[:, at:at + HEADS * PATCH * count].rearrange("p (h q t) -> p q t h", h=HEADS, q=PATCH)
                mask = seen[:, at // HEADS:at // HEADS + PATCH * count].rearrange("p (q t) -> p q t", q=PATCH)
                for part in range(3):
                    for r in range(2):
                        picked = banks[:, :, 48 * count * r:48 * count * (r + 1)].rearrange(
                            "p b (t k h) -> p b t k h", k=3, h=HEADS)[:, :, :, part, :]
                        other = (mask[:, 4 * r:4 * r + 4, :].unsqueeze(3).broadcast_to([128, 4, count, HEADS]) if part == 0
                                 else to[:, 4 * r:4 * r + 4])
                        last = nc.vector.tensor_tensor(to[:, 4 * r:4 * r + 4], picked, other, ALU.add)
                        if part < 2:
                            dve_steps[0] += 1
                            last.then_inc(s["dve_chain"], 1)
                        elif r:
                            last.then_inc(s["table_kept"], 1)
                    if part < 2:
                        dve.wait_ge(s["dve_chain"], dve_steps[0])
            dve.wait_ge(s["table_kept"], len(KINDS))

            def place_patches(k):
                r, (a, j, col) = PATCH_SOURCES[k]
                dve.wait_ge(s["turned"], k + 1)
                src = turned_bias(k).rearrange("p (r c) -> p r c", c=OUTER_W)[:, :, col:col + MIDDLE_W]
                slots = [(b, i) for b in range(2) for i in range(BIAS_PATCHES) if patch_source(b, i) == (r, (a, j, col))]
                for b, i in slots:
                    last = nc.vector.tensor_copy(biasp[:, b, i, :].rearrange("p (r c) -> p r c", c=MIDDLE_W), src)
                last.then_inc(s["placed"], 1)

            for k, (r, (a, j0, _)) in enumerate(PATCH_SOURCES):
                if k >= 8:
                    dve.wait_ge(s["turned"], k - 7)
                at = bias_at(a, OUTER_KINDS[r])
                nc.vector.tensor_copy(biasb[k % 8], bias[:, at:at + HEADS * PATCH * 3].rearrange(
                    "p (q t) -> p q t", t=3)[:, :, j0]).then_inc(s["rounded"], 1)
                if k >= 2:
                    place_patches(k - 2)
            for k in range(len(PATCH_SOURCES) - 2, len(PATCH_SOURCES)):
                place_patches(k)
            dve.wait_ge(s["placed"], len(PATCH_SOURCES))
            nc.vector.memset(small[:, 2, 0:1], 0.0).then_inc(s["init"], 1)
            dve.wait_ge(s["init"], INITS)

            def spread(j, c, heads):
                if heads[0] == 0:
                    if c % 2 == 0:
                        wait(dve, "lead", 3 * (c // 2) + 3, j)
                    if c:
                        wait(dve, "peak_in", CHUNK_BANKS * c, j)
                for h in heads:
                    last = nc.vector.tensor_scalar(Qbd[:, h, :, :], qparts[0].rearrange(
                        "p (a q t) -> p a q t", a=2, q=PATCH)[:, c % 2], cst[:, C_HEAD + h:C_HEAD + h + 1], None, ALU.mult)
                if heads[-1] == HEADS - 1:
                    last.then_inc(s["qbd"], 1)

            def maxima(j, c, b):
                first, count, _ = patch_bank(c % 2, b)
                wait(dve, "peak_in", CHUNK_BANKS * c + b + 1, j)
                if c and b == CHUNK_BANKS - 2:
                    wait(dve, "middle_in", 16 * c, j)
                nc.vector.tensor_reduce(out=mcol[:, first:first + count],
                                        in_=PS[:, PEAK, 0:PATCH_KEYS * count].rearrange("p (t k) -> p t k", k=PATCH_KEYS),
                                        axis=AX.X, op=ALU.max).then_inc(s["peak_out"], 1)

            def add_bias(j, c, n):
                cols = HEADS * PATCH * tile_of(c % 2, n)[1]
                T = TILES * c + n
                wait(dve, "scores", T + 1, j)
                wait(dve, "weighted", T - 3, j)
                at = bias_at(c % 2, n)
                nc.vector.tensor_tensor(S[:, n % 4, 0:cols], PS[:, SCORE + n % 2, 0:cols], bias[:, at:at + cols], ALU.add
                                        ).then_inc(s["biased"], 1)

            def select_heads(j, c, n):
                q = PATCH * tile_of(c % 2, n)[1]
                T = TILES * c + n
                wait(dve, "weighted", T + 1, j)
                wait(dve, "half", T - 1, j)
                src = PS[:, SUM + n % 2, 0:8 * q].rearrange("p (g h q) -> p g h q", g=2, h=4)
                mask = cst[:, C_OUT:C_OUT + 4].unsqueeze(1).unsqueeze(3).broadcast_to([128, 2, 4, q])
                nc.vector.tensor_tensor(masked[:, n % 2, 0:8 * q].rearrange("p (g h q) -> p g h q", g=2, h=4), src, mask,
                                        ALU.mult).then_inc(s["selected"], 1)

            def invert(j, c):
                wait(dve, "packed_in", 16 * (c + 1), j)
                nc.vector.reciprocal(packed[:, :], packed[:, :]).then_inc(s["recip"], 1)

            def divide(j, c):
                wait(dve, "den_in", 32 * (c + 1), j)
                wait(dve, "misc_in", misc_project(c - 1) + 1, j)
                nc.vector.tensor_tensor(normed[:, :], sel[:, (c + 1) % 2, :, :, :].rearrange("p g q t -> p (g q t)"),
                                        den[:, :], ALU.mult).then_inc(s["normed"], 1)

            spread(None, 0, spread_for(SPREAD, 0, False) + spread_for(SPREAD, 0, True))
            for b in range(CHUNK_BANKS):
                maxima(None, 0, b)
            next_image(None, 1, 1)
            spread(None, 1, spread_for(SPREAD, 1, False))
            add_bias(None, 0, 0)
            with nc.vector.Fori(0, IMAGES // 2) as j:
                for c in range(4):
                    for n in range(TILES):
                        add_bias(j, *((c, n + 1) if n + 1 < TILES else (c + 1, 0)))
                        if n > 1 or c:
                            select_heads(j, *((c, n - 2) if n > 1 else (c - 1, n - 2 + TILES)))
                        if n in SPREAD[c % 2]:
                            spread(j, c + 2 if n >= 12 else c + 1, SPREAD[c % 2][n])
                        if FIRST_BANK <= n < FIRST_BANK + CHUNK_BANKS:
                            maxima(j, c + 1, n - FIRST_BANK)
                        if n + TILES * (c % 2) == NEXT_IMAGE:
                            next_image(j, c // 2 + 2, (2 * j + c // 2 + 2) % IMAGES)
                        if n == RECIPROCAL:
                            invert(j, c)
                        if n == NORMALIZE:
                            divide(j, c)
                for n in range(TILES - 2, TILES):
                    select_heads(j, 3, n)
            invert(None, 2 * IMAGES)
            divide(None, 2 * IMAGES)

        @block.tensor
        def _(pe):
            mm = nc.tensor.matmul
            pe.wait_ge(s["const_in"], 16)
            with nc.tensor.Fori(0, IMAGES // X_RING) as j:
                for b in range(X_RING):
                    pe.wait_ge(s[f"xin_in{b}"], j * 16 + 16)
                    wait(pe, "xin_kept", b + 1 - X_RING, j, X_RING)
                    for k in range(PIECES):
                        o = PS[:, 2 * b + k // 4, PIECE * (k % 4):PIECE * (k % 4) + PIECE]
                        last = nc.tensor.transpose(o, xin[b][:, k, :], cst[0:PIECE, C_ID:C_ID + PIECE])
                    last.then_inc(s["xin_turned"], 1)

            def group_sums(k):
                pe.wait_ge(s["mean_in"], k + 1)
                mm(PS[:, PEAK, 0:IMAGES], group, mv[:, :, 0], start=True, stop=True).then_inc(s["mean_sum"], 1)
                pe.wait_ge(s["var_in"], k + 1)
                mm(PS[:, PEAK, 0:IMAGES], group, small[:, 2, :], start=True, stop=True).then_inc(s["var_sum"], 1)

            group_sums(0)
            with nc.tensor.Fori(0, IMAGES // 2) as j:
                for b in range(2):
                    pe.wait_ge(s["padded_ready"], j * 2 + b + 1)
                    image = padded[b].rearrange("p (r c) -> p r c", c=PAD)
                    for half in range(2):
                        wait(pe, "conv_added", 2 * b + half - 3, j, 4)
                        for tap in range(9):
                            r, c = tap // 3 + HALF_ROWS * half, tap % 3
                            last = mm(PS[:, 2 * b + half, 0:HALF], wconv[:, tap, :], image[:, r:r + HALF_ROWS, c:c + SIDE],
                                      start=tap == 0, stop=tap == 8)
                        last.then_inc(s["conv"], 1)
            group_sums(1)

            def project_qkv(j, i, which, half):
                k = misc_qkv(i, which, half)
                if which == KEY and half == 0:
                    wait(pe, "xn_ready", i + 1, j)
                if k > 1:
                    wait(pe, "misc_out", k - 1, j)
                weights = wqk[:, which, :] if which < VAL else wqkv[:, CH * VAL:CH * (VAL + 1)]
                mm(PS[:, MISC + k % 2, 0:HALF], weights, xn[:, HALF * half:HALF * half + HALF],
                   start=True, stop=True).then_inc(s["misc_in"], 1)

            pe.wait_ge(s["loaded"], SMALL_LOADS)
            pe.wait_ge(s["weights"], WEIGHTS)
            for which in (KEY, Q, VAL):
                for half in range(2):
                    project_qkv(None, 0, which, half)

            pe.wait_ge(s["table_split"], 2)
            for k, (a, n, at, count) in enumerate(KINDS):
                if k < 2:
                    wait(pe, "conv_added", 2 * IMAGES)
                    pe.wait_ge(s["sqrt_in"], 2)
                    wait(pe, "misc_out", MISC_FIRST)
                else:
                    pe.wait_ge(s["table_kept"], k - 1)
                for bank in range(4):
                    for r in range(2):
                        for j in range(count):
                            o = PS[:, 4 * (k % 2) + bank, 48 * (r * count + j):48 * (r * count + j) + 48]
                            first = selection_at(a, n, 4 * r + bank, j)
                            for i in range(2):
                                last = mm(o, chosen[i][0:TABLE_PARTS[i], first:first + 128], tparts[i],
                                          start=i == 0, stop=i == 1)
                last.then_inc(s["table_picked"], 1)
            pe.wait_ge(s["table_kept"], len(KINDS))
            for k in range(len(PATCH_SOURCES)):
                pe.wait_ge(s["rounded"], k + 1)
                if k >= 8:
                    pe.wait_ge(s["placed"], k - 7)
                nc.tensor.transpose(turned_bias(k), biasb[k % 8], identb[:, :]).then_inc(s["turned"], 1)

            def turn_values(j, c, n, w):
                if n == 0 and c % 2 == 0:
                    wait(pe, "misc_out", misc_qkv(c // 2, VAL, 1) + 1, j)
                if w:
                    wait(pe, "value_out", w, j)
                key = tile_of(c % 2, n)[3]
                nc.tensor.transpose(PS[:, VALUE, 0:128], V[c // 2 % 2][:, key:key + 128], ident
                                    ).then_inc(s["value_in"], 1)

            def score_tile(j, c, n):
                a, T = c % 2, TILES * c + n
                t0, count, key = tile_of(a, n)[:3]
                if n == 0:
                    wait(pe, "rows_in", ROWS_IN * (c + 1), j)
                if n == 2:
                    wait(pe, "middle_in", 16 * (c + 1), j)
                if T > 1:
                    wait(pe, "biased", T - 1, j)
                cols = 2 * PATCH * count
                for g in range(HEAD_PAIRS):
                    last = mm(PS[:, SCORE + n % 2, cols * g:cols * (g + 1)], key_rows[a][0:PEAK_ROW + 1, g, key:key + 128],
                              query_rows[a][0:PEAK_ROW + 1, g, :, :, t0:t0 + count], start=True, stop=True)
                last.then_inc(s["scores"], 1)

            def patch_scores(j, c, b):
                a = c % 2
                first, count, table_first = patch_bank(a, b)
                if b == 0:
                    wait(pe, "qbd", c + 1, j)
                    wait(pe, "qbd_too", c + 1, j)
                    if a == 0:
                        wait(pe, "lead", 3 * (c // 2) + 2, j)
                wait(pe, "peak_out", CHUNK_BANKS * c + b, j)
                mm(PS[:, PEAK, 0:PATCH_KEYS * count], identb[:, :], biasp[:, a, table_first:table_first + count, :],
                   start=True, stop=False)
                queries = Qbd.rearrange("p h q t -> p (h q) t")
                keys = k1[c // 2 % 2][:, CHUNK_KEYS * a:CHUNK_KEYS * (a + 1)]
                for i in range(count):
                    key, col, width = patch_keys(a, first + i)
                    rows = keys[:, key:key + 8 * width].rearrange("p (r c) -> p r c", c=width)
                    last = mm(PS[:, PEAK, PATCH_KEYS * i:PATCH_KEYS * (i + 1)], queries[:, :, first + i],
                              rows[:, :, col:col + MIDDLE_W], start=False, stop=i == count - 1)
                last.then_inc(s["peak_in"], 1)

            def weigh(j, c, n):
                T = TILES * c + n
                _, count, _, _, w = tile_of(c % 2, n)
                w += WINDOWS * c
                q = 4 * PATCH * count
                wait(pe, "probs", T + 1, j)
                if new_window(n) is not None:
                    wait(pe, "value_out", w + 1, j)
                wait(pe, "selected", T - 1, j)
                for g in range(4):
                    at = q * (g // 2)
                    last = mm(PS[64 * (g % 2):64 * (g % 2) + 64, SUM + n % 2, at:at + q], VT[:, w % 4, g, :],
                              S[:, n % 4, q * g:q * (g + 1)], start=True, stop=True)
                last.then_inc(s["weighted"], 1)

            def project_out(j, c, g):
                k = misc_project(c)
                if g == 0:
                    wait(pe, "normed", c + 1, j)
                    wait(pe, "misc_out", k - 1, j)
                last = mm(PS[:, MISC + k % 2, 0:CHUNK_Q], wproj[:, g, :], normed[:, CHUNK_Q * g:CHUNK_Q * (g + 1)],
                          start=g == 0, stop=g == 1)
                if g:
                    last.then_inc(s["misc_in"], 1)

            def turn_image(j, i, part):
                k = misc_turn(i, part)
                if part == 0:
                    wait(pe, "residual", i + 1, j)
                wait(pe, "misc_out", k - 1, j)
                for p in range(4 - part):
                    at = PIECE * (4 * part + p)
                    last = nc.tensor.transpose(PS[0:PIECE, MISC + k % 2, CH * p:CH * p + CH], yo[:, at:at + PIECE], ident)
                last.then_inc(s["misc_in"], 1)

            pe.wait_ge(s["init"], INITS)
            pe.wait_ge(s["cleared"], 4)
            pe.wait_ge(s["pool_loaded"], POOL_LOADS)
            turn_values(None, 0, 0, 0)
            for b in range(CHUNK_BANKS):
                patch_scores(None, 0, b)
            score_tile(None, 0, 0)
            score_tile(None, 0, 1)
            with nc.tensor.Fori(0, IMAGES // 2) as j:
                for c in range(4):
                    for n in range(TILES):
                        score_tile(j, *((c, n + 2) if n + 2 < TILES else (c + 1, n + 2 - TILES)))
                        window = window_for_next(c, n)
                        if window:
                            turn_values(j, *window)
                        if FIRST_BANK <= n < FIRST_BANK + CHUNK_BANKS:
                            patch_scores(j, c + 1, n - FIRST_BANK)
                        if MISC_PROJECT <= n < MISC_PROJECT + 2:
                            project_out(j, c, n - MISC_PROJECT)
                        step = n + TILES * (c % 2)
                        if step in PROJECTED:
                            project_qkv(j, c // 2 + 1, *PROJECTED[step])
                        if MISC_TURN <= step < MISC_TURN + 2:
                            turn_image(j, c // 2, step - MISC_TURN)
                        if n or c:
                            weigh(j, *((c, n - 1) if n else (c - 1, TILES - 1)))
                weigh(j, 3, TILES - 1)
            for g in range(2):
                project_out(None, 2 * IMAGES, g)
            for part in range(2):
                turn_image(None, IMAGES, part)


def kernel(x, L0_conv_W, L1_conv_w_qkv, L1_conv_b_qkv, L1_conv_rpb, L1_conv_w_proj, L1_conv_b_proj):
    import numpy as np
    import concourse.bacc as bacc
    from concourse.bass_utils import run_bass_kernel_spmd

    given = {
        "x": np.ascontiguousarray(x).reshape(IMAGES, POS, CH), "conv_w": np.ascontiguousarray(L0_conv_W),
        "w_qkv": np.ascontiguousarray(L1_conv_w_qkv), "b_qkv": np.ascontiguousarray(L1_conv_b_qkv),
        "rpb": np.ascontiguousarray(L1_conv_rpb), "w_proj": np.ascontiguousarray(L1_conv_w_proj),
        "b_proj": np.ascontiguousarray(L1_conv_b_proj),
    }
    given["const"], given["window"], given["select"] = constants()
    nc = bacc.Bacc("TRN2", target_bir_lowering=False, num_devices=1)
    aps = [nc.dram_tensor(n, a.shape, mybir.dt.from_np(a.dtype), kind="ExternalInput").ap() for n, a in given.items()]
    out = nc.dram_tensor("out", (IMAGES, POS, CH), mybir.dt.float32, kind="ExternalOutput").ap()
    build(nc, *aps, out)
    r = run_bass_kernel_spmd(nc, [given], core_ids=[0])
    return r.results[0]["out"].reshape(IMAGES, SIDE, SIDE, CH)
```
